# Optimizing a Trainium2 kernel written in Bass

```python
import numpy as np
import jax
import jax.numpy as jnp

def _softmax(x, axis=-1):
    return jax.nn.softmax(x, axis=axis)

def _gelu(x):
    return jax.nn.gelu(x, approximate=True)

def _silu(x):
    return jax.nn.silu(x)

def _sigmoid(x):
    return jax.nn.sigmoid(x)

def _layernorm(x, axis=-1, eps=1e-05):
    m = jnp.mean(x, axis=axis, keepdims=True)
    v = jnp.var(x, axis=axis, keepdims=True)
    return (x - m) / jnp.sqrt(v + eps)

def _scatter_add(tgt, idx, src, axis=0):
    return tgt.at[idx].add(src)

def _segment_sum(src, seg, n):
    return jax.ops.segment_sum(src, seg, n)
kernel_name = 'mk_prb_d1_jaxref_r4_38bd3c'

def setup_inputs(seed: int=0):
    np.random.seed(seed)
    _w = jnp.asarray

    def _L0_attn_setup():
        import jax, jax.numpy as jnp
        import numpy as np
        K_FACTOR = 0.5
        key = jax.random.key(seed)
        k1, k2, k3, k4 = jax.random.split(key, 4)
        B, S, H, I = (1, 512, 1024, 2752)
        x = jax.random.normal(k1, (B, S, H), dtype=jnp.float32)
        w_gate = jax.random.normal(k2, (I, H), dtype=jnp.float32) * 0.02
        w_up = jax.random.normal(k3, (I, H), dtype=jnp.float32) * 0.02
        w_down = jax.random.normal(k4, (H, I), dtype=jnp.float32) * 0.02
        return {'x': x, 'w_gate': w_gate, 'w_up': w_up, 'w_down': w_down}
    _L0_attn_in = _L0_attn_setup()

    def _L0_ffn_setup():
        import jax, jax.numpy as jnp
        import numpy as np
        HID, INT, LAT, NE, K = (1024, 2048, 512, 8, 2)
        LN_EPS = 1e-05

        def _layernorm(x, gamma, beta):
            mu = jnp.mean(x, axis=-1, keepdims=True)
            var = jnp.var(x, axis=-1, keepdims=True)
            return (x - mu) * jax.lax.rsqrt(var + LN_EPS) * gamma + beta
        key = jax.random.key(seed)
        ks = jax.random.split(key, 8)
        s = lambda d: 1.0 / np.sqrt(d)
        return {'hidden_states': jax.random.normal(ks[0], (4, 512, HID), jnp.float32), 'gate_w': jax.random.normal(ks[1], (HID, NE), jnp.float32) * s(HID), 'up_w': jax.random.normal(ks[2], (HID, INT), jnp.float32) * s(HID), 'down_w': jax.random.normal(ks[3], (INT, HID), jnp.float32) * s(INT), 'fc1_w': jax.random.normal(ks[4], (HID, LAT), jnp.float32) * s(HID), 'fc2_w': jax.random.normal(ks[5], (LAT, HID), jnp.float32) * s(LAT), 'expert_w': jax.random.normal(ks[6], (LAT, LAT), jnp.float32), 'ln_gamma': jnp.ones((HID,), jnp.float32), 'ln_beta': jnp.zeros((HID,), jnp.float32)}
    _L0_ffn_in = _L0_ffn_setup()
    _d = {'L0_attn_x': _L0_attn_in['x'], 'L0_attn_w_gate': _L0_attn_in['w_gate'], 'L0_attn_w_up': _L0_attn_in['w_up'], 'L0_attn_w_down': _L0_attn_in['w_down'], 'L0_ffn_gate_w': _L0_ffn_in['gate_w'], 'L0_ffn_up_w': _L0_ffn_in['up_w'], 'L0_ffn_down_w': _L0_ffn_in['down_w'], 'L0_ffn_fc1_w': _L0_ffn_in['fc1_w'], 'L0_ffn_fc2_w': _L0_ffn_in['fc2_w'], 'L0_ffn_expert_w': _L0_ffn_in['expert_w'], 'L0_ffn_ln_gamma': _L0_ffn_in['ln_gamma'], 'L0_ffn_ln_beta': _L0_ffn_in['ln_beta']}
    _x0 = _d['L0_attn_x']
    _d['L0_attn_x'] = jax.random.normal(jax.random.fold_in(jax.random.key(seed), 1), (4, 512, 1024), dtype=_x0.dtype)
    del _x0
    return _d

def reference(L0_attn_x, L0_attn_w_gate, L0_attn_w_up, L0_attn_w_down, L0_ffn_gate_w, L0_ffn_up_w, L0_ffn_down_w, L0_ffn_fc1_w, L0_ffn_fc2_w, L0_ffn_expert_w, L0_ffn_ln_gamma, L0_ffn_ln_beta):

    def _L0_attn_ref(x, w_gate, w_up, w_down):
        import jax, jax.numpy as jnp
        import numpy as np
        K_FACTOR = 0.5
        s = jax.nn.silu(jnp.einsum('bsh,ih->bsi', x, w_gate))
        B, S, I = s.shape
        k = int(K_FACTOR * I)
        _, idx = jax.lax.top_k(-jnp.abs(s), k)
        flat = s.reshape(B * S, I)
        rows = jnp.arange(B * S)[:, None]
        flat = flat.at[rows, idx.reshape(B * S, k)].set(0.0)
        s = flat.reshape(B, S, I)
        s = s * jnp.einsum('bsh,ih->bsi', x, w_up)
        return jnp.einsum('bsi,hi->bsh', s, w_down)

    def _L0_ffn_ref(hidden_states, gate_w, up_w, down_w, fc1_w, fc2_w, expert_w, ln_gamma, ln_beta):
        import jax, jax.numpy as jnp
        import numpy as np
        HID, INT, LAT, NE, K = (1024, 2048, 512, 8, 2)
        LN_EPS = 1e-05

        def _layernorm(x, gamma, beta):
            mu = jnp.mean(x, axis=-1, keepdims=True)
            var = jnp.var(x, axis=-1, keepdims=True)
            return (x - mu) * jax.lax.rsqrt(var + LN_EPS) * gamma + beta
        logits = jnp.einsum('bsh,he->bse', hidden_states, gate_w)
        routing_weights, selected_experts = jax.lax.top_k(logits, K)
        h = jax.nn.relu(jnp.einsum('bsh,hi->bsi', hidden_states, up_w)) ** 2
        shared_out = jnp.einsum('bsi,ih->bsh', h, down_w)
        x_latent = jnp.einsum('bsh,hl->bsl', hidden_states, fc1_w)
        expert_out = jnp.einsum('bsl,lm->bsm', x_latent, expert_w)
        moe_out = expert_out * jnp.sum(routing_weights, axis=-1, keepdims=True)
        routed_out = jnp.einsum('bsl,lh->bsh', moe_out, fc2_w)
        return _layernorm(shared_out + routed_out, ln_gamma, ln_beta)
    x = L0_attn_x
    xn = _layernorm(x, axis=-1)
    x = x + _L0_attn_ref(xn, L0_attn_w_gate, L0_attn_w_up, L0_attn_w_down) + _L0_ffn_ref(xn, L0_ffn_gate_w, L0_ffn_up_w, L0_ffn_down_w, L0_ffn_fc1_w, L0_ffn_fc2_w, L0_ffn_expert_w, L0_ffn_ln_gamma, L0_ffn_ln_beta)
    return x

_drawn_inputs = setup_inputs


def setup_inputs(seed=0):
    import zlib

    import numpy as np

    out = dict(_drawn_inputs(seed))
    spreads = {'L0_ffn_ln_gamma': (1.0, 0.2), 'L0_ffn_ln_beta': (0.0, 0.1)}
    factors = {}
    for name, (base, spread) in spreads.items():
        noise = np.random.default_rng([zlib.crc32(name.encode()), seed]).standard_normal(out[name].shape)
        drawn = base * np.exp(spread * noise) if base else spread * noise
        out[name] = jnp.asarray(drawn.astype(out[name].dtype))
    for name, factor in factors.items():
        out[name] = (out[name] * factor).astype(out[name].dtype)
    return out
```

```python
from contextlib import ExitStack

import numpy as np

import concourse.bass as bass
from concourse import mybir

F32 = mybir.dt.float32
F32R = mybir.dt.float32r
I32 = mybir.dt.int32
U8 = mybir.dt.uint8
BF16 = mybir.dt.bfloat16
I16 = mybir.dt.int16
ALU = mybir.AluOpType
ACT = mybir.ActivationFunctionType
AX = mybir.AxisListType

P = 128
N = 512
TOKENS, HID = 2048, 1024
GATED, SHARED, LATENT, EXPERTS = 2752, 2048, 512, 8
KEPT = GATED - GATED // 2
EPS = 1e-5

TILES = N // P
BLOCKS = TOKENS // N
HK = HID // P
LK = LATENT // P
GK = -(-GATED // P)
LAST = GATED - (GK - 1) * P
PAD = P - LAST
GC = -(-GATED // N)
GATE_TAIL = GATED - (GC - 1) * N
SC = SHARED // N
RING = 4
BITS = 31

STEPS = [(("gate", c), HK) for c in range(GC)]
STEPS += [(("latent", 0), HK), (("hidden", 0), HK), (("expert", 0), LK), (("hidden", 1), HK),
          (("routed", 0), LK), (("routed", 1), LK), (("shared", 0), HK), (("shared", 1), HK),
          (("hidden", 2), HK), (("hidden", 3), HK), (("shared", 2), HK), (("shared", 3), HK)]
STEPS += [(("up", c), HK) for c in range(GC)]
STEPS += [(("out", 0), GK), (("out", 1), GK)]
START, END, SET = {}, {}, {}
_m = 0
for _s, (_name, _n) in enumerate(STEPS):
    START[_name], END[_name], SET[_name] = _m, _m + _n - 1, _s % 2
    _m += _n
GRANULES = _m
ENDS = sorted(END.values())
INNER = GRANULES - len(STEPS)

TURN_AFTER = [5, 9, 13, 17]
AHEAD = 4

FILLED, USE = {}, {}
USES = [0] * 8


def _fill(key, bank):
    FILLED[key] = len(FILLED)
    USE[key] = (bank, USES[bank])
    USES[bank] += 1


for _name, _n in STEPS[:-2]:
    for _t in range(TILES):
        _fill((*_name, _t), 4 * SET[_name] + _t)
for _c in range(AHEAD):
    _fill(("turn", 0, _c), 4 + _c % 4)
for _k in range(GK):
    if _k + AHEAD < GK:
        _fill(("turn", 0, _k + AHEAD), 4 + (_k + AHEAD) % 4)
for _t in range(TILES):
    _fill(("out", 0, _t), _t)
for _t in range(TILES):
    for _h in range(2):
        _fill(("token", _t, _h), 2 * (_t % 2) + _h)
for _t in range(TILES):
    _fill(("out", 1, _t), 4 + _t)
FILLS = len(FILLED)
FIRST_FILLS = 2 * TILES
FIRST_USES = [2, 2, 2, 2, 0, 0, 0, 0]


def filled(b, key):
    return FIRST_FILLS + b * FILLS + FILLED[key] + 1


def emptied(b, key):
    bank, use = USE[key]
    return bank, 1 + FIRST_USES[bank] + b * USES[bank] + use + 1


def released(b, m):
    return RING + b * INNER + sum(1 for x in range(m + 1) if x not in ENDS)


READ_AT = {END[name] + RING: name for name, _ in STEPS if name[0] not in ("up", "out")}
READ_UP_AT = {END[("up", c)] + (RING if c < GC - 1 else 1): ("up", c) for c in range(GC)}
SEARCH_FROM = END[("gate", GC - 1)] + RING + 1
UP0, OUT0, OUT1 = START[("up", 0)], START[("out", 0)], START[("out", 1)]
SEARCH_AT = {SEARCH_FROM: 0}
while len(SEARCH_AT) < BITS:
    SEARCH_AT[max(SEARCH_AT) + (4 if max(SEARCH_AT) < UP0 else 3)] = len(SEARCH_AT)
SEARCH_END = max(SEARCH_AT) + 3
PRODUCT_AT = {max(SEARCH_END + 6 + g, END[("up", g)] + RING + 1): g for g in range(GC - 1)}
PRODUCT_AT[OUT0 + 1] = GC - 1
NORM_AT = [OUT0 + 2 + 3 * t for t in range(TILES)]
TOKENS_AT = [OUT0 + 18, OUT0 + 20, OUT1 + 10, OUT1 + 14]
RESIDUAL_LOAD = [UP0 + 8, UP0 + 9, NORM_AT[0] + 3, NORM_AT[1] + 3]
TOKENS_LOAD = [OUT0 + 14, OUT0 + 15, OUT1 + 7, OUT1 + 11]
VECTOR_TILES = (0, 1)
SCALAR_TILES = tuple(t for t in range(TILES) if t not in VECTOR_TILES)
NV, NS = len(VECTOR_TILES), len(SCALAR_TILES)


def searched(k):
    return 1 + k * (3 + NV)


SEARCHES = searched(BITS) + TILES + 4


def program(nc, x, w_gate, w_up, w_down, up_w, down_w, fc1_w, expert_w, fc2_w, gamma, beta, y):
    ctx = ExitStack()
    with ctx:
        def sb(name, shape, dt):
            return ctx.enter_context(nc.sbuf_tensor(name, shape, dt))

        def over(name, shape, dt, offset):
            return nc.alloc_sbuf_tensor_at(name, shape, dt, offset=offset)

        def sem(name):
            return ctx.enter_context(nc.semaphore(name))

        size = GK * TILES * P * 4
        base = -(-nc.sbuf_base // 32) * 32
        acc_at, a_at, u_at = base, base + TILES * HID * 4, base + TILES * HID * 4 + size
        u_size = 4 * HK * N * 4 // 2 + 2 * LK * N * 4
        sb("regions", [P, (TILES * HID * 4 + size + max(size, u_size)) // 4], F32)
        acc = over("acc", [P, TILES, HID], F32, acc_at)
        latent = [over(f"latent{i}", [P, LK, N], F32R, acc_at + i * LK * N * 4) for i in range(2)]
        mag = over("mag", [P, GK, TILES, P], F32, a_at)
        prod = over("prod", [P, GK, TILES, P], F32, u_at)
        prod_t = [over("prod_t0", [P, GK, N], F32R, a_at), over("prod_t1", [P, GK, N], F32R, u_at)]
        hidden = [over(f"hidden{i}", [P, HK, N], F32R, u_at + i * HK * N * 4) for i in range(2)]
        expert = [over(f"expert{i}", [P, LK, N], F32R, u_at + 2 * HK * N * 4 + i * LK * N * 4) for i in range(2)]

        tok = [sb(f"tok{i}", [P, HK, N], F32R) for i in range(2)]
        raw = sb("raw", [P, RING, N], F32)
        w = [sb(f"w{i}", [P, RING, N], F32R) for i in range(2)]
        positive = sb("positive", [P, GK, TILES, P], U8)
        rows = sb("rows", [P, 2, HID], F32)
        relu2 = rows[:, :, :].rearrange("p a (b n) -> p (a b) n", n=N)
        gamma_all = sb("gamma_all", [P, HID], F32)
        beta_all = sb("beta_all", [P, HID], F32)
        ident = sb("ident", [P, P], F32)
        junk_v = sb("junk_v", [P, GK, P], U8)
        junk_s = sb("junk_s", [P, GK, P], BF16)
        thr = sb("thr", [P, TILES], F32)
        cand = sb("cand", [P, TILES], F32)
        cnt = sb("cnt", [P, TILES], F32)
        step = sb("step", [P, TILES], F32)
        taken = sb("taken", [P, TILES], I32)
        extra = sb("extra", [P, TILES], F32)
        most = sb("most", [P, 32], F32)
        most_t = sb("most_t", [P, 32], F32)
        ties = sb("ties", [P, 1], I32)
        neg = sb("neg", [P, TILES], F32)
        top = sb("top", [P, TILES, 8], F32)
        route = sb("route", [P, TILES], F32)
        stats = sb("stats", [P, TILES, 2, 6], F32)
        mv = sb("mv", [P, TILES, 2], F32)
        var = sb("var", [P, TILES], F32)
        std = sb("std", [P, TILES], F32)
        rstd = sb("rstd", [P, TILES], F32)
        banks = [ctx.enter_context(nc.psum_tensor(f"bank{i}", [P, N], F32)) for i in range(8)]

        raw_loaded = [sem(f"raw_loaded{i}") for i in range(RING)]
        rows_loaded = [sem(f"rows_loaded{i}") for i in range(2)]
        consts_loaded = sem("consts_loaded")
        ident_ready = sem("ident_ready")
        hi_ready = sem("hi_ready")
        lo_ready = sem("lo_ready")
        granule_used = sem("granule_used")
        bank_filled = sem("bank_filled")
        bank_emptied = [sem(f"bank_emptied{i}") for i in range(8)]
        operand_hi = sem("operand_hi")
        hidden_lo = sem("hidden_lo")
        silu_done = sem("silu_done")
        signs_done = sem("signs_done")
        mag_ready = sem("mag_ready")
        route_ready = sem("route_ready")
        search = sem("search")
        counted = sem("counted")
        squared = sem("squared")
        kept = sem("kept")
        masked = sem("masked")
        constants_set = sem("constants_set")
        prod_ready = sem("prod_ready")
        norm_step = sem("norm_step")
        std_ready = sem("std_ready")
        apply_step = sem("apply_step")
        tokens_ready = sem("tokens_ready")
        stored = sem("stored")

        def source(m):
            name = max((s for s in START if START[s] <= m), key=lambda s: START[s])
            (kind, i), k = name, m - START[name]
            if kind in ("gate", "up"):
                width = N if i < GC - 1 else GATE_TAIL + (EXPERTS if kind == "gate" else 0)
                src = w_gate if kind == "gate" else w_up
                return src[k * P:(k + 1) * P, i * N:i * N + width], P, width
            if kind == "latent":
                return fc1_w[k * P:(k + 1) * P, :], P, N
            if kind == "expert":
                return expert_w[k * P:(k + 1) * P, :], P, N
            if kind == "hidden":
                return up_w[k * P:(k + 1) * P, i * N:(i + 1) * N], P, N
            if kind == "routed":
                return fc2_w[k * P:(k + 1) * P, i * N:(i + 1) * N], P, N
            if kind == "shared":
                k += HK * (i // 2)
                return down_w[k * P:(k + 1) * P, i % 2 * N:(i % 2 + 1) * N], P, N
            n = P if k < GK - 1 else LAST
            return w_down[k * P:k * P + n, i * N:(i + 1) * N], n, N

        def rows_of(t):
            return rows[:, t % 2, :]

        block = ctx.enter_context(nc.Block())

        @block.sync
        def _(sp):
            def load_granule(m):
                src, n, width = source(m % GRANULES)
                sp.dma_start(raw[0:n, m % RING, 0:width], src).then_inc(raw_loaded[m % RING], 16)

            def load_rows(b, t):
                sp.dma_start(rows_of(t), x[bass.ds(((b % BLOCKS) * TILES + t) * P, P), :])\
                  .then_inc(rows_loaded[t % 2], 16)

            for t in range(2):
                load_rows(0, t)
            sp.dma_start(gamma_all[:, :], gamma.to_broadcast([P, HID])).then_inc(consts_loaded, 16)
            sp.dma_start(beta_all[:, :], beta.to_broadcast([P, HID])).then_inc(consts_loaded, 16)
            for m in range(RING):
                load_granule(m)
            for t in range(2, TILES):
                sp.wait_ge(bank_filled, 2 * (t - 2) + 2)
                load_rows(0, t)
            with sp.Fori(0, BLOCKS) as b:
                for m in range(GRANULES):
                    sp.wait_ge(lo_ready, b * GRANULES + m + 1)
                    load_granule(m + RING)
                    for t in range(TILES):
                        if m == RESIDUAL_LOAD[t]:
                            if t < 2:
                                sp.wait_ge(hidden_lo, (b + 1) * SC * TILES + 1)
                            else:
                                sp.wait_ge(apply_step, b * 4 * TILES + 4 * (t - 1))
                            load_rows(b, t)
                        if m == TOKENS_LOAD[t]:
                            if t < 2:
                                sp.wait_ge(apply_step, b * 4 * TILES + 4 * (t + 3))
                            else:
                                sp.wait_ge(bank_filled, filled(b, ("token", t - 2, 1)))
                            load_rows(b + 1, t)
                for t in range(TILES):
                    bank, value = emptied(b, ("out", 1, t))
                    sp.wait_ge(bank_emptied[bank], value)
                    bank, value = emptied(b, ("out", 0, t))
                    sp.wait_ge(bank_emptied[bank], value)
                    sp.dma_start(y[bass.ds((b * TILES + t) * P, P), :], acc[:, t, :]).then_inc(stored, 16)
            for i in range(RING):
                sp.wait_ge(raw_loaded[i], 16 * (BLOCKS * GRANULES // RING + 1))
            sp.wait_ge(stored, 16 * (TILES * BLOCKS + 1))

        @block.gpsimd
        def _(pool):
            pool.memset(ident[:, :], 0.0).then_inc(ident_ready, 1)
            pool.wait_ge(ident_ready, 1)
            pool.affine_select(out=ident[:, :], in_=ident[:, :], compare_op=ALU.not_equal, fill=1.0,
                               base=0, pattern=[[-1, P]], channel_multiplier=1).then_inc(ident_ready, 1)
            with pool.Fori(0, BLOCKS) as b:
                for m in range(GRANULES):
                    _, n, width = source(m)
                    r = m % RING
                    pool.wait_ge(hi_ready, b * GRANULES + m + 1)
                    pool.tensor_tensor(w[1][0:n, r, 0:width], raw[0:n, r, 0:width], w[0][0:n, r, 0:width],
                                       ALU.subtract).then_inc(lo_ready, 1)

        @block.scalar
        def _(act):
            def split(b, m):
                _, n, width = source(m)
                r = m % RING
                act.wait_ge(raw_loaded[r], 16 * (b * (GRANULES // RING) + m // RING + 1))
                before = m - RING
                if before < 0:
                    if before == -1:
                        act.wait_ge(bank_filled, FIRST_FILLS + b * FILLS)
                    else:
                        act.wait_ge(granule_used, b * INNER + RING + before + 2)
                elif before in ENDS:
                    name = next(s for s in END if END[s] == before)
                    act.wait_ge(bank_filled, filled(b, (*name, TILES - 1)))
                else:
                    act.wait_ge(granule_used, released(b, before))
                act.activation(w[0][0:n, r, 0:width], raw[0:n, r, 0:width], ACT.Copy).then_inc(hi_ready, 1)

            def standard(e, t):
                act.wait_ge(norm_step, 5 * e + 5)
                act.activation(std[:, t:t + 1], var[:, t:t + 1], ACT.Sqrt).then_inc(std_ready, 1)

            def count(b, k, n, t):
                act.wait_ge(search, b * SEARCHES + searched(k) + 1)
                if k or n:
                    act.wait_ge(counted, (b * BITS + k) * NS + n)
                act.activation(junk_s[:, :, :], mag[:, :, t, :], ACT.Sign, scale=-1.0,
                               bias=cand[:, t:t + 1], accum_out=cnt[:, t:t + 1]).then_inc(counted, 1)

            def turn_tokens(t, fills):
                for h in range(2):
                    act.wait_ge(bank_filled, fills[h])
                    half = HK // 2
                    act.activation(tok[0][:, h * half:(h + 1) * half, t * P:(t + 1) * P],
                                   banks[2 * (t % 2) + h][:, :].rearrange("p (k n) -> p k n", n=P),
                                   ACT.Copy).then_inc(operand_hi, 1)

            def read_step(b, name):
                kind, i = name
                if kind == "latent":
                    act.wait_ge(stored, 16 * (b * TILES + 1))
                if kind == "routed" and i == 0:
                    act.wait_ge(route_ready, b + 1)
                for t in range(TILES):
                    bank = USE[(*name, t)][0]
                    if kind == "gate":
                        act.wait_ge(bank_filled, filled(b, (*name, t)))
                        if i < GC - 1:
                            act.activation(mag[:, 4 * i:4 * i + 4, t, :],
                                           banks[bank][:, :].rearrange("p (k n) -> p k n", n=P),
                                           ACT.Silu).then_inc(bank_emptied[bank], 1)
                        else:
                            act.activation(mag[:, GK - 2, t, :], banks[bank][:, 0:P], ACT.Silu).then_inc(silu_done, 1)
                            act.activation(mag[:, GK - 1, t, 0:LAST], banks[bank][:, P:P + LAST],
                                           ACT.Silu).then_inc(silu_done, 1)
                    if kind in ("latent", "expert"):
                        act.wait_ge(bank_filled, filled(b, (*name, t)))
                        to = latent if kind == "latent" else expert
                        act.activation(to[0][:, t, :], banks[bank][:, :], ACT.Copy).then_inc(operand_hi, 1)
                    if kind == "hidden":
                        if t == 0:
                            act.wait_ge(hidden_lo, b * SC * TILES + i * TILES + 1)
                        act.wait_ge(bank_filled, filled(b, (*name, t)))
                        act.activation(relu2[:, t, :], banks[bank][:, :], ACT.Relu).then_inc(bank_emptied[bank], 1)
                        act.wait_ge(bank_emptied[bank], emptied(b, (*name, t))[1])
                        act.activation(hidden[0][:, i % 2 * TILES + t, :], relu2[:, t, :],
                                       ACT.Square).then_inc(operand_hi, 1)
                    if kind == "routed":
                        act.wait_ge(bank_filled, filled(b, (*name, t)))
                        act.activation(acc[:, t, i * N:(i + 1) * N], banks[bank][:, :], ACT.Copy,
                                       scale=route[:, t:t + 1]).then_inc(bank_emptied[bank], 1)

            act.sem_inc(stored, 16)
            for t in range(TILES):
                standard(t, t)
                turn_tokens(t, [2 * t + 1, 2 * t + 2])
            with act.Fori(0, BLOCKS) as b:
                for m in range(GRANULES):
                    split(b, m)
                    if m in READ_AT:
                        read_step(b, READ_AT[m])
                    for n, t in enumerate(SCALAR_TILES):
                        if m - n in SEARCH_AT:
                            count(b, SEARCH_AT[m - n], n, t)
                    for t in range(TILES):
                        if m == NORM_AT[t]:
                            standard(TILES + 8 * b + t, t)
                        if m == TOKENS_AT[t]:
                            standard(TILES + 8 * b + TILES + t, t)
                        if m == OUT1 + TURN_AFTER[t] + RING:
                            turn_tokens(t, [filled(b, ("token", t, h)) for h in range(2)])
                    if OUT0 <= m < OUT0 + GK:
                        c = m - OUT0
                        n = P if c < GK - 1 else LAST
                        act.wait_ge(bank_filled, filled(b, ("turn", 0, c)))
                        act.activation(prod_t[0][0:n, c, :], banks[4 + c % 4][0:n, :], ACT.Copy).then_inc(operand_hi, 1)

        @block.tensor
        def _(pe):
            def product(out, left, right, first, last):
                pe.matmul(out, left[0], right[0], start=first, stop=False)
                pe.matmul(out, left[0], right[1], start=False, stop=False)
                return pe.matmul(out, left[1], right[0], start=False, stop=last)

            def wait_bank(b, key):
                bank, value = emptied(b, key)
                pe.wait_ge(bank_emptied[bank], value - 1)

            def turn_token(t):
                for h in range(2):
                    for k in range(HK // 2):
                        last = pe.transpose(banks[2 * (t % 2) + h][:, k * P:(k + 1) * P],
                                            rows_of(t)[:, (h * HK // 2 + k) * P:(h * HK // 2 + k + 1) * P], ident[:, :])
                    last.then_inc(bank_filled, 1)

            def turn_product(b, c):
                wait_bank(b, ("turn", 0, c))
                if c % 4 == 0:
                    pe.wait_ge(prod_ready, b * GC + c // 4 + 1)
                for t in range(TILES):
                    last = pe.transpose(banks[4 + c % 4][:, t * P:(t + 1) * P], prod[:, c, t, :], ident[:, :])
                last.then_inc(bank_filled, 1)

            def granule(b, name, k, count):
                kind, i = name
                m = START[name] + k
                _, n, width = source(m)
                r = m % RING
                pe.wait_ge(lo_ready, b * GRANULES + m + 1)
                if kind == "gate" and i == 0 and k == 0:
                    for t in range(TILES):
                        pe.wait_ge(bank_emptied[t], 1 + FIRST_USES[t] + b * USES[t])
                if kind == "expert":
                    bank, value = emptied(b, ("latent", 0, k))
                    pe.wait_ge(bank_emptied[bank], value)
                if kind == "routed":
                    bank, value = emptied(b, ("expert", 0, k))
                    pe.wait_ge(bank_emptied[bank], value)
                if kind == "shared":
                    pe.wait_ge(hidden_lo, b * SC * TILES + HK * (i // 2) + k + 2)
                if kind == "out" and i == 0:
                    bank, value = emptied(b, ("turn", 0, k))
                    pe.wait_ge(bank_emptied[bank], value)
                right = [part[0:n, r, 0:width] for part in w]
                for t in range(TILES):
                    if k == 0:
                        wait_bank(b, (*name, t))
                    out = banks[USE[(*name, t)][0]]
                    s = slice(t * P, (t + 1) * P)
                    if kind in ("gate", "up"):
                        last = product(out[:, 0:width], [p[:, k, s] for p in tok], right, k == 0, k == count - 1)
                    elif kind in ("latent", "hidden"):
                        last = product(out[:, :], [p[:, r, s] for p in w], [p[:, k, :] for p in tok],
                                       k == 0, k == count - 1)
                    elif kind == "expert":
                        last = product(out[:, :], [p[:, r, s] for p in w], [p[:, k, :] for p in latent],
                                       k == 0, k == count - 1)
                    else:
                        left = {"routed": expert, "shared": hidden, "out": prod_t}[kind]
                        last = product(out[:, :], [p[0:n, k, s] for p in left], right, k == 0, k == count - 1)
                    if k == count - 1:
                        last.then_inc(bank_filled, 1)
                if k < count - 1:
                    last.then_inc(granule_used, 1)

            for s in bank_emptied:
                pe.sem_inc(s, 1)
            pe.sem_inc(granule_used, RING)
            pe.wait_ge(ident_ready, 2)
            for t in range(TILES):
                pe.wait_ge(tokens_ready, t + 1)
                if t >= 2:
                    for h in range(2):
                        pe.wait_ge(bank_emptied[2 * (t % 2) + h], 2)
                turn_token(t)
            with pe.Fori(0, BLOCKS) as b:
                for name, count in STEPS:
                    if name == ("out", 0):
                        for c in range(AHEAD):
                            turn_product(b, c)
                    for k in range(count):
                        granule(b, name, k, count)
                        if name == ("out", 0) and k + AHEAD < GK:
                            turn_product(b, k + AHEAD)
                        if name == ("out", 1) and k in TURN_AFTER:
                            t = TURN_AFTER.index(k)
                            pe.wait_ge(tokens_ready, TILES * (b + 1) + t + 1)
                            for h in range(2):
                                wait_bank(b, ("token", t, h))
                            turn_token(t)

        @block.vector
        def _(dve):
            def moments(e, t, src):
                dve.wait_ge(norm_step, 5 * e + 1)
                for h in range(2):
                    dve.bn_stats(stats[:, t, h, :], src[:, h * N:(h + 1) * N]).then_inc(norm_step, 1)
                dve.drain()
                dve.bn_aggr(mv[:, t, :], stats[:, t, :, :]).then_inc(norm_step, 1)
                dve.wait_ge(norm_step, 5 * e + 4)
                dve.tensor_scalar(var[:, t:t + 1], mv[:, t, 1:2], EPS, None, ALU.add).then_inc(norm_step, 1)

            def inverse(e, t):
                dve.wait_ge(std_ready, e + 1)
                dve.reciprocal(rstd[:, t:t + 1], std[:, t:t + 1]).then_inc(norm_step, 1)
                dve.wait_ge(norm_step, 5 * e + 6)

            def normalise(e, t, loads):
                dve.wait_ge(rows_loaded[t % 2], 16 * loads)
                moments(e, t, rows_of(t))
                inverse(e, t)
                dve.tensor_scalar(rows_of(t), rows_of(t), mv[:, t, 0:1], rstd[:, t:t + 1], ALU.subtract,
                                  ALU.mult).then_inc(tokens_ready, 1)

            def turn_tokens(t, highs):
                for h in range(2):
                    half = HK // 2
                    bank = 2 * (t % 2) + h
                    s = slice(t * P, (t + 1) * P)
                    dve.wait_ge(operand_hi, highs + h + 1)
                    dve.tensor_tensor(tok[1][:, h * half:(h + 1) * half, s],
                                      banks[bank][:, :].rearrange("p (k n) -> p k n", n=P),
                                      tok[0][:, h * half:(h + 1) * half, s], ALU.subtract).then_inc(bank_emptied[bank], 1)

            HIGHS = 2 * LK + SC * TILES + GK + 2 * TILES

            def highs(b, kind, n):
                first = {"latent": 0, "hidden0": LK, "expert": LK + TILES, "hidden": 2 * LK + TILES,
                         "turn": 2 * LK + SC * TILES, "token": 2 * LK + SC * TILES + GK}[kind]
                return 2 * TILES + b * HIGHS + first + n

            def read_gate(b, c):
                if c < GC - 1:
                    for t in range(TILES):
                        bank, value = emptied(b, ("gate", c, t))
                        dve.wait_ge(bank_emptied[bank], value)
                    parts = [(slice(4 * c, 4 * c + 4), slice(0, P))]
                else:
                    dve.wait_ge(silu_done, (b + 1) * 2 * TILES)
                    parts = [(GK - 2, slice(0, P)), (GK - 1, slice(0, LAST))]
                for i, (ks, ns) in enumerate(parts):
                    dve.tensor_scalar(positive[:, ks, :, ns], mag[:, ks, :, ns], 0.0, 2.0, ALU.is_ge,
                                      ALU.mult).then_inc(signs_done, 1)
                    dve.wait_ge(signs_done, b * (GC + 1) + c + i + 1)
                    bits = mag[:, ks, :, ns].bitcast(I32)
                    dve.tensor_scalar(bits, bits, 0x7FFFFFFF, None, ALU.bitwise_and).then_inc(mag_ready, 1)

            def read_logits(b):
                for t in range(TILES):
                    bank = USE[("gate", GC - 1, t)][0]
                    dve.max(top[:, t, :], banks[bank][:, GATE_TAIL:GATE_TAIL + EXPERTS]).then_inc(bank_emptied[bank], 1)
                for t in range(TILES):
                    bank, value = emptied(b, ("gate", GC - 1, t))
                    dve.wait_ge(bank_emptied[bank], value)
                dve.tensor_tensor(route[:, :], top[:, :, 0], top[:, :, 1], ALU.add).then_inc(route_ready, 1)

            def read_step(b, name):
                kind, i = name
                if kind == "gate":
                    read_gate(b, i)
                    if i == GC - 1:
                        read_logits(b)
                        dve.memset(mag[:, GK - 1, :, LAST:P], -1.0).then_inc(mag_ready, 1)
                for t in range(TILES):
                    key = (*name, t)
                    bank, value = USE[key][0], emptied(b, key)[1]
                    cols = slice(i % 2 * N, (i % 2 + 1) * N)
                    if kind in ("latent", "expert"):
                        to = latent if kind == "latent" else expert
                        dve.wait_ge(operand_hi, highs(b, kind, t + 1))
                        dve.tensor_tensor(to[1][:, t, :], banks[bank][:, :], to[0][:, t, :],
                                          ALU.subtract).then_inc(bank_emptied[bank], 1)
                    if kind == "shared":
                        dve.wait_ge(bank_filled, filled(b, key))
                        over_bank, over_value = emptied(b, ("routed" if i < 2 else "shared", i % 2, t))
                        dve.wait_ge(bank_emptied[over_bank], over_value)
                        dve.tensor_tensor(acc[:, t, cols], banks[bank][:, :], acc[:, t, cols],
                                          ALU.add).then_inc(bank_emptied[bank], 1)
                    if kind == "up":
                        dve.wait_ge(bank_filled, filled(b, key))
                        if i < GC - 1:
                            dve.scalar_tensor_tensor(out=prod[:, 4 * i:4 * i + 4, t, :],
                                                     in0=positive[:, 4 * i:4 * i + 4, t, :], scalar=-1.0,
                                                     in1=banks[bank][:, :].rearrange("p (k n) -> p k n", n=P),
                                                     op0=ALU.add, op1=ALU.mult).then_inc(bank_emptied[bank], 1)
                        else:
                            dve.scalar_tensor_tensor(out=prod[:, GK - 2, t, :], in0=positive[:, GK - 2, t, :],
                                                     scalar=-1.0, in1=banks[bank][:, 0:P],
                                                     op0=ALU.add, op1=ALU.mult).then_inc(kept, 1)
                            dve.scalar_tensor_tensor(out=prod[:, GK - 1, t, 0:LAST],
                                                     in0=positive[:, GK - 1, t, 0:LAST], scalar=-1.0,
                                                     in1=banks[bank][:, P:P + LAST],
                                                     op0=ALU.add, op1=ALU.mult).then_inc(bank_emptied[bank], 1)
                if kind == "up" and i == GC - 1:
                    dve.memset(prod[:, GK - 1, :, LAST:P], 0.0).then_inc(kept, 1)
                if kind == "hidden":
                    for t in range(TILES):
                        n = i % 2 * TILES + t
                        dve.wait_ge(operand_hi, highs(b, "hidden0" if i == 0 else "hidden",
                                                      t + 1 if i == 0 else (i - 1) * TILES + t + 1))
                        dve.tensor_tensor(relu2[:, t, :], relu2[:, t, :], relu2[:, t, :], ALU.mult).then_inc(squared, 1)
                        dve.wait_ge(squared, b * SC * TILES + i * TILES + t + 1)
                        dve.tensor_tensor(hidden[1][:, n, :], relu2[:, t, :], hidden[0][:, n, :],
                                          ALU.subtract).then_inc(hidden_lo, 1)

            KEPT_STEPS = TILES + 1

            def settle(b, k):
                at = b * SEARCHES + searched(k) + 1 + NV
                dve.wait_ge(counted, (b * BITS + k + 1) * NS)
                dve.wait_ge(search, at)
                dve.scalar_tensor_tensor(out=step[:, :], in0=cnt[:, :], scalar=float(PAD + 1), in1=cand[:, :],
                                         op0=ALU.is_le, op1=ALU.mult).then_inc(search, 1)
                dve.wait_ge(search, at + 1)
                dve.tensor_tensor(thr[:, :], thr[:, :], step[:, :], ALU.max).then_inc(search, 1)
                dve.wait_ge(search, at + 2)

            def search_bit(b, k):
                at = b * SEARCHES + searched(k)
                dve.wait_ge(search, at)
                dve.tensor_scalar(cand[:, :].bitcast(I32), thr[:, :].bitcast(I32), 1 << (BITS - 1 - k), None,
                                  ALU.bitwise_or).then_inc(search, 1)
                for i, t in enumerate(VECTOR_TILES):
                    dve.wait_ge(search, at + 1 + i)
                    dve.tensor_scalar(junk_v[:, :, :], mag[:, :, t, :], cand[:, t:t + 1], float(1 - (GATED - KEPT)),
                                      ALU.is_lt, ALU.add, accum_out=cnt[:, t:t + 1]).then_inc(search, 1)

            def drop_ties(b):
                at = b * SEARCHES + searched(BITS)
                for t in range(TILES):
                    dve.wait_ge(search, at + t)
                    dve.tensor_scalar(junk_v[:, :, :], mag[:, :, t, :], thr[:, t:t + 1], None, ALU.is_ge, ALU.add,
                                      accum_out=cnt[:, t:t + 1]).then_inc(search, 1)
                dve.wait_ge(search, at + TILES)
                dve.tensor_scalar(extra[:, :], cnt[:, :], -float(KEPT), None, ALU.add).then_inc(search, 1)
                dve.wait_ge(search, at + TILES + 1)
                dve.tensor_reduce(most[:, 0:1], extra[:, :], AX.X, ALU.max).then_inc(search, 1)
                dve.wait_ge(search, at + TILES + 2)
                dve.transpose(most_t[:, :], most[:, :]).then_inc(search, 1)
                dve.wait_ge(search, at + TILES + 3)
                dve.tensor_reduce(ties[:, :], most_t[:, :], AX.X, ALU.max).then_inc(search, 1)
                dve.drain()
                excess = sum(dve.value_load(ties[q:q + 1, 0:1], min_val=0, max_val=GATED) for q in range(0, P, 32))
                with dve.If(excess > 0):
                    dve.scalar_tensor_tensor(out=cand[:, :], in0=thr[:, :], scalar=0.7 * 2.0 ** -23, in1=thr[:, :],
                                             op0=ALU.mult, op1=ALU.add)
                    for t in range(TILES):
                        dve.drain()
                        dve.tensor_scalar(junk_v[:, :, :], mag[:, :, t, :], cand[:, t:t + 1], None, ALU.is_ge,
                                          ALU.add, accum_out=cnt[:, t:t + 1])
                    dve.drain()
                    dve.tensor_scalar(taken[:, :], cnt[:, :], float(KEPT), None, ALU.is_ge)
                    dve.tensor_scalar(neg[:, :], cnt[:, :], -float(KEPT), None, ALU.add)
                    dve.drain()
                    dve.copy_predicated(thr[:, :], taken[:, :], cand[:, :])
                    dve.copy_predicated(extra[:, :], taken[:, :], neg[:, :])
                    dve.drain()
                    dve.tensor_scalar(neg[:, :], thr[:, :], -1.0, None, ALU.mult)
                    equal = junk_v[:, :, :].rearrange("p k n -> p (k n)")
                    rank = junk_s[:, :, :].bitcast(I16).rearrange("p k n -> p (k n)")
                    for t in range(TILES):
                        dve.drain()
                        dve.tensor_scalar(junk_v[:, :, :], mag[:, :, t, :], thr[:, t:t + 1], None, ALU.is_equal)
                        dve.drain()
                        dve.tensor_tensor_scan(rank, equal, equal, 0.0, ALU.add, ALU.max)
                        dve.drain()
                        dve.scalar_tensor_tensor(out=equal, in0=rank, scalar=extra[:, t:t + 1], in1=equal,
                                                 op0=ALU.is_le, op1=ALU.mult)
                        dve.drain()
                        dve.scalar_tensor_tensor(out=mag[:, :, t, :], in0=junk_v[:, :, :], scalar=neg[:, t:t + 1],
                                                 in1=mag[:, :, t, :], op0=ALU.mult, op1=ALU.add)
                    dve.drain()

            def gated_product(b, g):
                ks = slice(4 * g, min(4 * g + 4, GK))
                at = b * KEPT_STEPS
                for t in range(TILES):
                    bank, value = emptied(b, ("up", g, t))
                    dve.wait_ge(bank_emptied[bank], value)
                    if g == GC - 1:
                        dve.wait_ge(kept, at + TILES + 1)
                    dve.scalar_tensor_tensor(out=prod[:, ks, t, :], in0=mag[:, ks, t, :], scalar=thr[:, t:t + 1],
                                             in1=prod[:, ks, t, :], op0=ALU.is_ge, op1=ALU.mult)\
                       .then_inc(masked, 1)
                dve.wait_ge(masked, (b * GC + g + 1) * TILES)
                dve.tensor_tensor(prod[:, ks, :, :], prod[:, ks, :, :], mag[:, ks, :, :], ALU.mult).then_inc(prod_ready, 1)

            def add_out(b, i):
                for t in range(TILES):
                    bank = USE[("out", i, t)][0]
                    dve.wait_ge(bank_filled, filled(b, ("out", i, t)))
                    dve.wait_ge(apply_step, (b * TILES + t + 1) * 4)
                    dve.tensor_tensor(acc[:, t, i * N:(i + 1) * N], banks[bank][:, :], acc[:, t, i * N:(i + 1) * N],
                                      ALU.add).then_inc(bank_emptied[bank], 1)

            def apply_norm(b, t):
                at = (b * TILES + t) * 4
                dve.tensor_scalar(acc[:, t, :], acc[:, t, :], mv[:, t, 0:1], rstd[:, t:t + 1], ALU.subtract,
                                  ALU.mult).then_inc(apply_step, 1)
                dve.wait_ge(apply_step, at + 1)
                dve.tensor_tensor(acc[:, t, :], acc[:, t, :], gamma_all[:, :], ALU.mult).then_inc(apply_step, 1)
                dve.wait_ge(apply_step, at + 2)
                dve.tensor_tensor(acc[:, t, :], acc[:, t, :], beta_all[:, :], ALU.add).then_inc(apply_step, 1)
                dve.wait_ge(apply_step, at + 3)
                dve.wait_ge(rows_loaded[t % 2], 16 * (2 + 4 * b + t // 2 + 1))
                dve.tensor_tensor(acc[:, t, :], acc[:, t, :], rows_of(t), ALU.add).then_inc(apply_step, 1)

            dve.sem_inc(norm_step, 1)
            dve.sem_inc(hidden_lo, 1)
            dve.memset(most[:, :], 0.0).then_inc(constants_set, 1)
            dve.wait_ge(constants_set, 1)
            for t in range(TILES):
                normalise(t, t, t // 2 + 1)
                turn_tokens(t, 2 * t)
            dve.wait_ge(consts_loaded, 32)
            with dve.Fori(0, BLOCKS) as b:
                for m in range(GRANULES):
                    if m in READ_AT:
                        read_step(b, READ_AT[m])
                    if m in READ_UP_AT:
                        read_step(b, READ_UP_AT[m])
                    if m == SEARCH_FROM:
                        dve.wait_ge(mag_ready, (b + 1) * (GC + 2))
                        dve.memset(thr[:, :], 0.0).then_inc(search, 1)
                    if m in SEARCH_AT:
                        if SEARCH_AT[m]:
                            settle(b, SEARCH_AT[m] - 1)
                        search_bit(b, SEARCH_AT[m])
                    if m == SEARCH_END:
                        settle(b, BITS - 1)
                        drop_ties(b)
                    if m in PRODUCT_AT:
                        gated_product(b, PRODUCT_AT[m])
                    for t in range(TILES):
                        if m == NORM_AT[t]:
                            for i in (2, 3):
                                bank, value = emptied(b, ("shared", i, t))
                                dve.wait_ge(bank_emptied[bank], value)
                            moments(TILES + 8 * b + t, t, acc[:, t, :])
                        if m == NORM_AT[t] + 2:
                            inverse(TILES + 8 * b + t, t)
                            apply_norm(b, t)
                        if m == TOKENS_AT[t]:
                            normalise(TILES + 8 * b + TILES + t, t, 2 + 4 * b + 2 + t // 2 + 1)
                        if m == OUT1 + TURN_AFTER[t] + RING:
                            turn_tokens(t, highs(b, "token", 2 * t))
                    if OUT0 <= m < OUT0 + GK:
                        c = m - OUT0
                        n = P if c < GK - 1 else LAST
                        bank = 4 + c % 4
                        dve.wait_ge(operand_hi, highs(b, "turn", c + 1))
                        dve.tensor_tensor(prod_t[1][0:n, c, :], banks[bank][0:n, :], prod_t[0][0:n, c, :],
                                          ALU.subtract).then_inc(bank_emptied[bank], 1)
                    if m == OUT1 + RING:
                        add_out(b, 0)
                add_out(b, 1)


def kernel(**inputs):
    import concourse.bacc as bacc
    from concourse.bass_utils import run_bass_kernel_spmd

    a = {k: np.asarray(v) for k, v in inputs.items()}
    arrays = {
        "x": np.ascontiguousarray(a["L0_attn_x"].reshape(TOKENS, HID)),
        "w_gate": np.ascontiguousarray(np.concatenate([a["L0_attn_w_gate"].T, a["L0_ffn_gate_w"]], axis=1)),
        "w_up": np.ascontiguousarray(a["L0_attn_w_up"].T),
        "w_down": np.ascontiguousarray(a["L0_attn_w_down"].T),
        "up_w": a["L0_ffn_up_w"], "down_w": a["L0_ffn_down_w"], "fc1_w": a["L0_ffn_fc1_w"],
        "expert_w": a["L0_ffn_expert_w"], "fc2_w": a["L0_ffn_fc2_w"],
        "gamma": a["L0_ffn_ln_gamma"].reshape(1, HID), "beta": a["L0_ffn_ln_beta"].reshape(1, HID),
    }
    nc = bacc.Bacc("TRN2", target_bir_lowering=False, num_devices=1)
    args = [nc.dram_tensor(f"{k}_dram", v.shape, F32, kind="ExternalInput").ap() for k, v in arrays.items()]
    y = nc.dram_tensor("y_dram", (TOKENS, HID), F32, kind="ExternalOutput").ap()
    program(nc, *args, y)
    r = run_bass_kernel_spmd(nc, [{f"{k}_dram": np.ascontiguousarray(v) for k, v in arrays.items()}], core_ids=[0])
    return r.results[0]["y_dram"].reshape(a["L0_attn_x"].shape)
```

```python
from contextlib import ExitStack

import numpy as np

import concourse.bass as bass
from concourse import mybir

F32 = mybir.dt.float32
F32R = mybir.dt.float32r
I32 = mybir.dt.int32
U8 = mybir.dt.uint8
BF16 = mybir.dt.bfloat16
I16 = mybir.dt.int16
ALU = mybir.AluOpType
ACT = mybir.ActivationFunctionType
AX = mybir.AxisListType

P = 128
N = 512
TOKENS, HID = 2048, 1024
GATED, SHARED, LATENT, EXPERTS = 2752, 2048, 512, 8
KEPT = GATED - GATED // 2
EPS = 1e-5

TILES = N // P
BLOCKS = TOKENS // N
HK = HID // P
LK = LATENT // P
GK = -(-GATED // P)
LAST = GATED - (GK - 1) * P
PAD = P - LAST
GC = -(-GATED // N)
TAIL = GATED - (GC - 1) * N
SC = SHARED // N
RING = 4
BITS = 31

STEPS = [(("gate", c), HK) for c in range(GC)]
STEPS += [(("latent", 0), HK), (("hidden", 0), HK), (("hidden", 1), HK),
          (("routed", 0), LK), (("routed", 1), LK), (("shared", 0), HK), (("shared", 1), HK),
          (("hidden", 2), HK), (("hidden", 3), HK), (("shared", 2), HK), (("shared", 3), HK)]
STEPS += [(("up", c), HK) for c in range(GC - 1)]
STEPS += [(("out", 0), GK), (("out", 1), GK)]
START, END, SET = {}, {}, {}
_m = 0
for _s, (_name, _n) in enumerate(STEPS):
    START[_name], END[_name], SET[_name] = _m, _m + _n - 1, _s % 2
    _m += _n
GRANULES = _m
ENDS = sorted(END.values())
INNER = GRANULES - len(STEPS)

TURN_AFTER = [5, 9, 13, 17]
AHEAD = 4
TURN_LEAD = 5

FILLED, USE = {}, {}
USES = [0] * 8


def _fill(key, bank):
    FILLED[key] = len(FILLED)
    USE[key] = (bank, USES[bank])
    USES[bank] += 1


for _name, _n in STEPS[:-2]:
    if _name == ("up", GC - 2):
        for _c in range(AHEAD):
            _fill(("turn", 0, _c), _c)
    for _t in range(TILES):
        _fill((*_name, _t), 4 * SET[_name] + _t)
for _k in range(GK):
    if _k + AHEAD < GK:
        _fill(("turn", 0, _k + AHEAD), 4 + (_k + AHEAD) % 4)
for _t in range(TILES):
    _fill(("out", 0, _t), _t)
for _t in range(TILES):
    for _h in range(2):
        _fill(("token", _t, _h), 2 * (_t % 2) + _h)
for _t in range(TILES):
    _fill(("out", 1, _t), 4 + _t)
FILLS = len(FILLED)
FIRST = [("token", 0), ("token", 1), ("weights", 0), ("token", 2), ("token", 3), ("weights", 1)]
FIRST_AT, _m = {}, 0
for _key in FIRST:
    FIRST_AT[_key] = _m
    _m += 2 if _key[0] == "token" else LK
FIRST_FILLS = _m
FIRST_USES = [2, 2, 2, 2, 2, 2, 2, 2]


def filled(b, key):
    return FIRST_FILLS + b * FILLS + FILLED[key] + 1


def emptied(b, key):
    bank, use = USE[key]
    return bank, 1 + FIRST_USES[bank] + b * USES[bank] + use + 1


def released(b, m):
    return RING + b * INNER + sum(1 for x in range(m + 1) if x not in ENDS)


UP0, OUT0, OUT1 = START[("up", 0)], START[("out", 0)], START[("out", 1)]
HIGH_FROM = {"latent": 0, "hidden": LK, "turn": LK + SC * TILES, "token": LK + SC * TILES + GK}
HIGHS = LK + SC * TILES + GK + 2 * TILES


def highs(b, kind, n):
    return 2 * TILES + b * HIGHS + HIGH_FROM[kind] + n


READ_AT = {END[name] + RING: name for name, _ in STEPS if name[0] not in ("up", "out")}
READ_UP_AT = {END[("up", c)] + (RING if c < GC - 2 else 1): ("up", c) for c in range(GC - 1)}
SEARCH_AT = {END[("gate", GC - 1)] + RING + 1: 0}
while len(SEARCH_AT) < BITS:
    _last = max(SEARCH_AT)
    SEARCH_AT[_last + (3 if _last >= UP0 or len(SEARCH_AT) % 2 else 4)] = len(SEARCH_AT)
SEARCH_FROM, SEARCH_END = min(SEARCH_AT), max(SEARCH_AT) + 3
MASK_AT = {SEARCH_END + 1: 0, SEARCH_END + 2: 1, SEARCH_END + 3: 2, SEARCH_END + 4: GC - 1}
MASK_AT[max(SEARCH_END + 5, END[("up", 3)] + RING + 1)] = 3
MASK_AT[OUT0 + 2] = 4
GATED_AT = {OUT0 - TURN_LEAD + c: c for c in range(GK)}
TURNED_AT = {OUT0 - TURN_LEAD + 3 + c: c for c in range(AHEAD)}
TURNED_AT.update({OUT0 + c: c for c in range(AHEAD, GK)})
assert len(GATED_AT) == GK and len(MASK_AT) == GC
SQUARE_AT = {END[("hidden", i)] + RING + t: (i, t) for i in range(SC) for t in range(TILES)}
GPSIMD_HI = [m for m in range(SEARCH_FROM, OUT0) if m % 3 == 1]
NORM_AT = [OUT0 + 2 + 3 * t for t in range(TILES)]
TOKENS_AT = [OUT0 + 18, OUT0 + 20, OUT1 + 10, OUT1 + 14]
RESIDUAL_LOAD = [UP0 + 10, UP0 + 11, NORM_AT[0] + 3, NORM_AT[1] + 3]
TOKENS_LOAD = [OUT0 + 14, OUT0 + 15, OUT1 + 7, OUT1 + 11]
VECTOR_TILES = (0, 1)
SCALAR_TILES = tuple(t for t in range(TILES) if t not in VECTOR_TILES)
NV, NS = len(VECTOR_TILES), len(SCALAR_TILES)


def scalar_his(b, m):
    return b * (GRANULES - len(GPSIMD_HI)) + sum(1 for x in range(m + 1) if x not in GPSIMD_HI)


def ring_slot_free(eng, raw_loaded, granule_used, bank_filled, b, m):
    eng.wait_ge(raw_loaded[m % RING], 16 * (b * (GRANULES // RING) + m // RING + 1))
    before = m - RING
    if before == -1:
        eng.wait_ge(bank_filled, FIRST_FILLS + b * FILLS)
    elif before < 0:
        eng.wait_ge(granule_used, b * INNER + RING + before + 2)
    elif before in ENDS:
        name = next(s for s in END if END[s] == before)
        eng.wait_ge(bank_filled, filled(b, (*name, TILES - 1)))
    else:
        eng.wait_ge(granule_used, released(b, before))


def searched(k):
    return 1 + k * (3 + NV)


SEARCHES = searched(BITS) + TILES + 4


def program(nc, x, w_gate, w_up, w_down, up_w, down_w, fc1_w, expert_w, fc2_w, gamma, beta, routed_w, y):
    ctx = ExitStack()
    with ctx:
        def sb(name, shape, dt):
            return ctx.enter_context(nc.sbuf_tensor(name, shape, dt))

        def over(name, shape, dt, offset):
            return nc.alloc_sbuf_tensor_at(name, shape, dt, offset=offset)

        def sem(name):
            return ctx.enter_context(nc.semaphore(name))

        size = GK * TILES * P * 4
        acc_at = -(-nc.sbuf_base // 32) * 32
        a_at = acc_at + TILES * HID * 4
        u_at = a_at + size
        rows_at = u_at + size
        sb("regions", [P, (TILES * HID * 4 + 2 * size + 2 * HID * 4) // 4], F32)
        acc = over("acc", [P, TILES, HID], F32, acc_at)
        rows = over("rows", [P, 2, HID], F32, rows_at)
        mag = over("mag", [P, GK, TILES, P], F32, a_at)
        prod = over("prod", [P, GK, TILES, P], F32, u_at)
        prod_t = [over("prod_t0", [P, GK, N], F32R, a_at), over("prod_t1", [P, GK, N], F32R, u_at)]
        hidden = [over(f"hidden{i}", [P, HK, N], F32R, u_at + i * HK * N * 4) for i in range(2)]
        squares = over("squares", [P, HK, N], F32, u_at + HK * N * 4)
        latent = [over("latent0", [P, LK, N], F32R, u_at + 2 * HK * N * 4), over("latent1", [P, LK, N], F32R, rows_at)]
        assert 2 * HK * N + LK * N <= (GK - 2) * TILES * P
        expert_raw = over("expert_raw", [P, LK, N], F32, a_at)
        fc2_raw = over("fc2_raw", [P, LK, HID], F32, a_at + LK * N * 4)
        expert = [over(f"expert{i}", [P, LK, N], F32R, a_at + (3 + i) * LK * N * 4) for i in range(2)]
        fc2 = [over(f"fc2_{i}", [P, LK, HID], F32R, u_at + i * LK * HID * 4) for i in range(2)]

        tok = [sb(f"tok{i}", [P, HK, N], F32R) for i in range(2)]
        raw = sb("raw", [P, RING, N], F32)
        w = [sb(f"w{i}", [P, RING, N], F32R) for i in range(2)]
        positive = sb("positive", [P, GK, TILES, P], U8)
        gamma_all = sb("gamma_all", [P, HID], F32)
        beta_all = sb("beta_all", [P, HID], F32)
        ident = sb("ident", [P, P], F32)
        junk_v = sb("junk_v", [P, GK, P], U8)
        junk_s = sb("junk_s", [P, GK, P], BF16)
        thr = sb("thr", [P, TILES], F32)
        cand = sb("cand", [P, TILES], F32)
        cnt = sb("cnt", [P, TILES], F32)
        step = sb("step", [P, TILES], F32)
        taken = sb("taken", [P, TILES], I32)
        extra = sb("extra", [P, TILES], F32)
        most = sb("most", [P, 32], F32)
        most_t = sb("most_t", [P, 32], F32)
        ties = sb("ties", [P, 1], I32)
        neg = sb("neg", [P, TILES], F32)
        top = sb("top", [P, TILES, 8], F32)
        route = sb("route", [P, TILES], F32)
        stats = sb("stats", [P, TILES, 2, 6], F32)
        mv = sb("mv", [P, TILES, 2], F32)
        var = sb("var", [P, TILES], F32)
        std = sb("std", [P, TILES], F32)
        rstd = sb("rstd", [P, TILES], F32)
        banks = [ctx.enter_context(nc.psum_tensor(f"bank{i}", [P, N], F32)) for i in range(8)]

        raw_loaded = [sem(f"raw_loaded{i}") for i in range(RING)]
        rows_loaded = [sem(f"rows_loaded{i}") for i in range(2)]
        consts_loaded = sem("consts_loaded")
        ident_ready = sem("ident_ready")
        hi_ready = sem("hi_ready")
        lo_ready = sem("lo_ready")
        granule_used = sem("granule_used")
        bank_filled = sem("bank_filled")
        bank_emptied = [sem(f"bank_emptied{i}") for i in range(8)]
        operand_hi = sem("operand_hi")
        hidden_lo = sem("hidden_lo")
        silu_done = sem("silu_done")
        signs_done = sem("signs_done")
        mag_ready = sem("mag_ready")
        route_ready = sem("route_ready")
        search = sem("search")
        counted = sem("counted")
        squared = sem("squared")
        gpsimd_hi = sem("gpsimd_hi")
        gpsimd_turn = sem("gpsimd_turn")
        first_loaded = sem("first_loaded")
        first_hi = sem("first_hi")
        first_lo = sem("first_lo")
        routed_stored = sem("routed_stored")
        kept = sem("kept")
        masked = sem("masked")
        constants_set = sem("constants_set")
        prod_ready = sem("prod_ready")
        norm_step = sem("norm_step")
        std_ready = sem("std_ready")
        apply_step = sem("apply_step")
        tokens_ready = sem("tokens_ready")
        stored = sem("stored")

        def source(m):
            name = max((s for s in START if START[s] <= m), key=lambda s: START[s])
            (kind, i), k = name, m - START[name]
            if kind in ("gate", "up"):
                width = N if i < GC - 1 else TAIL + EXPERTS + TAIL
                src = w_gate if kind == "gate" else w_up
                return src[k * P:(k + 1) * P, i * N:i * N + width], P, width
            if kind == "latent":
                return fc1_w[k * P:(k + 1) * P, :], P, N
            if kind == "hidden":
                return up_w[k * P:(k + 1) * P, i * N:(i + 1) * N], P, N
            if kind == "routed":
                return routed_w[k * P:(k + 1) * P, i * N:(i + 1) * N], P, N
            if kind == "shared":
                k += HK * (i // 2)
                return down_w[k * P:(k + 1) * P, i % 2 * N:(i % 2 + 1) * N], P, N
            n = P if k < GK - 1 else LAST
            return w_down[k * P:k * P + n, i * N:(i + 1) * N], n, N

        def rows_of(t):
            return rows[:, t % 2, :]

        block = ctx.enter_context(nc.Block())

        @block.sync
        def _(sp):
            def load_granule(m):
                src, n, width = source(m % GRANULES)
                if m == START[("routed", 0)]:
                    sp.wait_ge(routed_stored, 16)
                sp.dma_start(raw[0:n, m % RING, 0:width], src).then_inc(raw_loaded[m % RING], 16)

            def load_rows(b, t):
                sp.dma_start(rows_of(t), x[bass.ds(((b % BLOCKS) * TILES + t) * P, P), :])\
                  .then_inc(rows_loaded[t % 2], 16)

            for t in range(2):
                load_rows(0, t)
            sp.dma_start(expert_raw[:, :, :], expert_w.rearrange("(k p) n -> p k n", p=P)).then_inc(first_loaded, 16)
            sp.dma_start(fc2_raw[:, :, :], fc2_w.rearrange("(k p) n -> p k n", p=P)).then_inc(first_loaded, 16)
            sp.dma_start(gamma_all[:, :], gamma.to_broadcast([P, HID])).then_inc(consts_loaded, 16)
            sp.dma_start(beta_all[:, :], beta.to_broadcast([P, HID])).then_inc(consts_loaded, 16)
            for m in range(RING):
                load_granule(m)
            for t in range(2, TILES):
                sp.wait_ge(bank_filled, FIRST_AT[("token", t - 2)] + 2)
                load_rows(0, t)
            for t in range(LK):
                sp.wait_ge(bank_emptied[4 + t], 1 + FIRST_USES[4 + t])
            sp.dma_start(routed_w.rearrange("(k p) n -> p k n", p=P), acc[:, :, :]).then_inc(routed_stored, 16)
            with sp.Fori(0, BLOCKS) as b:
                for m in range(GRANULES):
                    sp.wait_ge(lo_ready, b * GRANULES + m + 1)
                    load_granule(m + RING)
                    for t in range(TILES):
                        if m == RESIDUAL_LOAD[t]:
                            if t < 2:
                                sp.wait_ge(bank_filled, filled(b, ("routed", 1, TILES - 1)))
                            else:
                                sp.wait_ge(apply_step, b * 4 * TILES + 4 * (t - 1))
                            load_rows(b, t)
                        if m == TOKENS_LOAD[t]:
                            if t < 2:
                                sp.wait_ge(apply_step, b * 4 * TILES + 4 * (t + 3))
                            else:
                                sp.wait_ge(bank_filled, filled(b, ("token", t - 2, 1)))
                            load_rows(b + 1, t)
                for t in range(TILES):
                    bank, value = emptied(b, ("out", 1, t))
                    sp.wait_ge(bank_emptied[bank], value)
                    bank, value = emptied(b, ("out", 0, t))
                    sp.wait_ge(bank_emptied[bank], value)
                    sp.dma_start(y[bass.ds((b * TILES + t) * P, P), :], acc[:, t, :]).then_inc(stored, 16)
            for i in range(RING):
                sp.wait_ge(raw_loaded[i], 16 * (BLOCKS * GRANULES // RING + 1))
            sp.wait_ge(stored, 16 * (TILES * BLOCKS + 1))

        @block.gpsimd
        def _(pool):
            pool.memset(ident[:, :], 0.0).then_inc(ident_ready, 1)
            pool.wait_ge(ident_ready, 1)
            pool.affine_select(out=ident[:, :], in_=ident[:, :], compare_op=ALU.not_equal, fill=1.0,
                               base=0, pattern=[[-1, P]], channel_multiplier=1).then_inc(ident_ready, 1)
            for k in range(LK):
                pool.wait_ge(first_hi, 2 * k + 1)
                pool.tensor_tensor(expert[1][:, k, :], expert_raw[:, k, :], expert[0][:, k, :],
                                   ALU.subtract).then_inc(first_lo, 1)
                pool.wait_ge(first_hi, 2 * k + 2)
                for h in range(2):
                    s = slice(h * N, (h + 1) * N)
                    pool.tensor_tensor(fc2[1][:, k, s], fc2_raw[:, k, s], fc2[0][:, k, s],
                                       ALU.subtract).then_inc(first_lo, 1)
            with pool.Fori(0, BLOCKS) as b:
                for m in range(GRANULES):
                    _, n, width = source(m)
                    r = m % RING
                    words, hi, lo = (v[0:n, r, 0:width] for v in (raw, *w))
                    if m in GPSIMD_HI:
                        ring_slot_free(pool, raw_loaded, granule_used, bank_filled, b, m)
                        pool.sem_inc(gpsimd_turn, 1)
                        pool.tensor_scalar(hi, words, 1.0, 1.0, ALU.mult, ALU.mult).then_inc(gpsimd_hi, 1)
                        pool.wait_ge(gpsimd_hi, b * len(GPSIMD_HI) + GPSIMD_HI.index(m) + 1)
                    else:
                        pool.wait_ge(hi_ready, scalar_his(b, m))
                    pool.tensor_tensor(lo, words, hi, ALU.subtract).then_inc(lo_ready, 1)
                    if m in SQUARE_AT:
                        i, t = SQUARE_AT[m]
                        pool.wait_ge(operand_hi, highs(b, "hidden", i * TILES + t + 1))
                        n = i % 2 * TILES + t
                        pool.tensor_tensor(squares[:, n, :], squares[:, n, :], squares[:, n, :],
                                           ALU.mult).then_inc(squared, 1)
                    if m in GATED_AT:
                        c = GATED_AT[m]
                        pool.wait_ge(masked, (b * GC + c // 4 + 1) * TILES)
                        pool.tensor_tensor(prod[:, c, :, :], prod[:, c, :, :], mag[:, c, :, :],
                                           ALU.mult).then_inc(prod_ready, 1)

        @block.scalar
        def _(act):
            def split(b, m):
                _, n, width = source(m)
                r = m % RING
                ring_slot_free(act, raw_loaded, granule_used, bank_filled, b, m)
                act.activation(w[0][0:n, r, 0:width], raw[0:n, r, 0:width], ACT.Copy).then_inc(hi_ready, 1)

            def standard(e, t):
                act.wait_ge(norm_step, 5 * e + 5)
                act.activation(std[:, t:t + 1], var[:, t:t + 1], ACT.Sqrt).then_inc(std_ready, 1)

            def count(b, k, n, t):
                act.wait_ge(search, b * SEARCHES + searched(k) + 1)
                if k or n:
                    act.wait_ge(counted, (b * BITS + k) * NS + n)
                act.activation(junk_s[:, :, :], mag[:, :, t, :], ACT.Sign, scale=-1.0,
                               bias=cand[:, t:t + 1], accum_out=cnt[:, t:t + 1]).then_inc(counted, 1)

            def turn_tokens(t, fills):
                for h in range(2):
                    act.wait_ge(bank_filled, fills[h])
                    half = HK // 2
                    act.activation(tok[0][:, h * half:(h + 1) * half, t * P:(t + 1) * P],
                                   banks[2 * (t % 2) + h][:, :].rearrange("p (k n) -> p k n", n=P),
                                   ACT.Copy).then_inc(operand_hi, 1)

            def read_step(b, name):
                kind, i = name
                if kind == "routed" and i == 0:
                    act.wait_ge(stored, 16 * (b * TILES + 1))
                    act.wait_ge(route_ready, (b + 1) * (TILES + 1))
                for t in range(TILES):
                    bank = USE[(*name, t)][0]
                    if kind == "gate":
                        act.wait_ge(bank_filled, filled(b, (*name, t)))
                        if i < GC - 1:
                            act.activation(mag[:, 4 * i:4 * i + 4, t, :],
                                           banks[bank][:, :].rearrange("p (k n) -> p k n", n=P),
                                           ACT.Silu).then_inc(bank_emptied[bank], 1)
                        else:
                            act.activation(mag[:, GK - 2, t, :], banks[bank][:, 0:P], ACT.Silu).then_inc(silu_done, 1)
                            act.activation(mag[:, GK - 1, t, 0:LAST], banks[bank][:, P:P + LAST],
                                           ACT.Silu).then_inc(silu_done, 1)
                    if kind == "latent":
                        act.wait_ge(bank_filled, filled(b, (*name, t)))
                        act.activation(latent[0][:, t, :], banks[bank][:, :], ACT.Copy).then_inc(operand_hi, 1)
                    if kind == "hidden":
                        n = i % 2 * TILES + t
                        act.wait_ge(bank_filled, filled(b, (*name, t)))
                        act.activation(squares[:, n, :], banks[bank][:, :], ACT.Relu).then_inc(bank_emptied[bank], 1)
                        act.wait_ge(bank_emptied[bank], emptied(b, (*name, t))[1])
                        act.activation(hidden[0][:, n, :], squares[:, n, :],
                                       ACT.Square).then_inc(operand_hi, 1)
                    if kind == "routed":
                        act.wait_ge(bank_filled, filled(b, (*name, t)))
                        act.activation(acc[:, t, i * N:(i + 1) * N], banks[bank][:, :], ACT.Copy,
                                       scale=route[:, t:t + 1]).then_inc(bank_emptied[bank], 1)

            act.sem_inc(stored, 16)

            def first_parts(k):
                act.wait_ge(first_loaded, 32)
                act.activation(expert[0][:, k, :], expert_raw[:, k, :], ACT.Copy).then_inc(first_hi, 1)
                act.activation(fc2[0][:, k, :], fc2_raw[:, k, :], ACT.Copy).then_inc(first_hi, 1)

            def first_copy(h):
                for t in range(LK):
                    act.wait_ge(bank_filled, FIRST_AT[("weights", h)] + t + 1)
                    act.activation(acc[:, t, h * N:(h + 1) * N], banks[4 + t][:, :], ACT.Copy).then_inc(bank_emptied[4 + t], 1)

            def first_tokens(t):
                turn_tokens(t, [FIRST_AT[("token", t)] + 1, FIRST_AT[("token", t)] + 2])

            standard(0, 0)
            first_parts(0)
            first_parts(1)
            standard(1, 1)
            first_tokens(0)
            first_parts(2)
            first_parts(3)
            first_tokens(1)
            standard(2, 2)
            standard(3, 3)
            first_copy(0)
            first_tokens(2)
            first_tokens(3)
            first_copy(1)
            with act.Fori(0, BLOCKS) as b:
                for m in range(GRANULES):
                    if m not in GPSIMD_HI:
                        split(b, m)
                    if m in READ_AT:
                        read_step(b, READ_AT[m])
                    for n, t in enumerate(SCALAR_TILES):
                        if m - n in SEARCH_AT:
                            count(b, SEARCH_AT[m - n], n, t)
                    for t in range(TILES):
                        if m == NORM_AT[t]:
                            standard(TILES + 8 * b + t, t)
                        if m == TOKENS_AT[t]:
                            standard(TILES + 8 * b + TILES + t, t)
                        if m == OUT1 + TURN_AFTER[t] + RING:
                            turn_tokens(t, [filled(b, ("token", t, h)) for h in range(2)])
                    if m in TURNED_AT:
                        c = TURNED_AT[m]
                        n = P if c < GK - 1 else LAST
                        act.wait_ge(bank_filled, filled(b, ("turn", 0, c)))
                        act.activation(prod_t[0][0:n, c, :], banks[USE[("turn", 0, c)][0]][0:n, :], ACT.Copy).then_inc(operand_hi, 1)

        @block.tensor
        def _(pe):
            def product(out, left, right, first, last):
                pe.matmul(out, left[0], right[0], start=first, stop=False)
                pe.matmul(out, left[0], right[1], start=False, stop=False)
                return pe.matmul(out, left[1], right[0], start=False, stop=last)

            def wait_bank(b, key):
                bank, value = emptied(b, key)
                pe.wait_ge(bank_emptied[bank], value - 1)

            def turn_token(t):
                for h in range(2):
                    for k in range(HK // 2):
                        last = pe.transpose(banks[2 * (t % 2) + h][:, k * P:(k + 1) * P],
                                            rows_of(t)[:, (h * HK // 2 + k) * P:(h * HK // 2 + k + 1) * P], ident[:, :])
                    last.then_inc(bank_filled, 1)

            def turn_product(b, c):
                bank = USE[("turn", 0, c)][0]
                wait_bank(b, ("turn", 0, c))
                pe.wait_ge(prod_ready, b * GK + c + 1)
                for t in range(TILES):
                    last = pe.transpose(banks[bank][:, t * P:(t + 1) * P], prod[:, c, t, :], ident[:, :])
                last.then_inc(bank_filled, 1)

            def granule(b, name, k, count):
                kind, i = name
                m = START[name] + k
                _, n, width = source(m)
                r = m % RING
                pe.wait_ge(lo_ready, b * GRANULES + m + 1)
                if kind == "gate" and i == 0 and k == 0:
                    for t in range(TILES):
                        pe.wait_ge(bank_emptied[t], 1 + FIRST_USES[t] + b * USES[t])
                if kind == "routed" and i == 0:
                    bank, value = emptied(b, ("latent", 0, k))
                    pe.wait_ge(bank_emptied[bank], value)
                if kind == "shared":
                    pe.wait_ge(hidden_lo, b * SC * TILES + HK * (i // 2) + k + 2)
                if kind == "out" and i == 0:
                    bank, value = emptied(b, ("turn", 0, k))
                    pe.wait_ge(bank_emptied[bank], value)
                right = [part[0:n, r, 0:width] for part in w]
                for t in range(TILES):
                    if k == 0:
                        wait_bank(b, (*name, t))
                    out = banks[USE[(*name, t)][0]]
                    s = slice(t * P, (t + 1) * P)
                    if kind in ("gate", "up"):
                        last = product(out[:, 0:width], [p[:, k, s] for p in tok], right, k == 0, k == count - 1)
                    elif kind in ("latent", "hidden"):
                        last = product(out[:, :], [p[:, r, s] for p in w], [p[:, k, :] for p in tok],
                                       k == 0, k == count - 1)
                    else:
                        left = {"routed": latent, "shared": hidden, "out": prod_t}[kind]
                        last = product(out[:, :], [p[0:n, k, s] for p in left], right, k == 0, k == count - 1)
                    if k == count - 1:
                        last.then_inc(bank_filled, 1)
                if k < count - 1:
                    last.then_inc(granule_used, 1)

            for s in bank_emptied:
                pe.sem_inc(s, 1)
            pe.sem_inc(granule_used, RING)
            pe.wait_ge(ident_ready, 2)
            for kind, i in FIRST:
                if kind == "token":
                    pe.wait_ge(tokens_ready, i + 1)
                    if i >= 2:
                        for h in range(2):
                            pe.wait_ge(bank_emptied[2 * (i % 2) + h], 2)
                    turn_token(i)
                else:
                    for k in range(LK):
                        pe.wait_ge(first_lo, 3 * k + 2 + i)
                        for t in range(LK):
                            if k == 0 and i:
                                pe.wait_ge(bank_emptied[4 + t], 2)
                            last = product(banks[4 + t][:, :], [p[:, k, t * P:(t + 1) * P] for p in expert],
                                           [p[:, k, i * N:(i + 1) * N] for p in fc2], k == 0, k == LK - 1)
                            if k == LK - 1:
                                last.then_inc(bank_filled, 1)
            with pe.Fori(0, BLOCKS) as b:
                for name, count in STEPS:
                    for k in range(count):
                        granule(b, name, k, count)
                        if 0 <= START[name] + k - (OUT0 - TURN_LEAD) < AHEAD:
                            turn_product(b, START[name] + k - (OUT0 - TURN_LEAD))
                        if name == ("out", 0) and k + AHEAD < GK:
                            turn_product(b, k + AHEAD)
                        if name == ("out", 1) and k in TURN_AFTER:
                            t = TURN_AFTER.index(k)
                            pe.wait_ge(tokens_ready, TILES * (b + 1) + t + 1)
                            for h in range(2):
                                wait_bank(b, ("token", t, h))
                            turn_token(t)

        @block.vector
        def _(dve):
            def moments(e, t, src):
                dve.wait_ge(norm_step, 5 * e + 1)
                for h in range(2):
                    dve.bn_stats(stats[:, t, h, :], src[:, h * N:(h + 1) * N]).then_inc(norm_step, 1)
                dve.drain()
                dve.bn_aggr(mv[:, t, :], stats[:, t, :, :]).then_inc(norm_step, 1)
                dve.wait_ge(norm_step, 5 * e + 4)
                dve.tensor_scalar(var[:, t:t + 1], mv[:, t, 1:2], EPS, None, ALU.add).then_inc(norm_step, 1)

            def inverse(e, t):
                dve.wait_ge(std_ready, e + 1)
                dve.reciprocal(rstd[:, t:t + 1], std[:, t:t + 1]).then_inc(norm_step, 1)
                dve.wait_ge(norm_step, 5 * e + 6)

            def normalise(e, t, loads):
                dve.wait_ge(rows_loaded[t % 2], 16 * loads)
                moments(e, t, rows_of(t))
                inverse(e, t)
                dve.tensor_scalar(rows_of(t), rows_of(t), mv[:, t, 0:1], rstd[:, t:t + 1], ALU.subtract,
                                  ALU.mult).then_inc(tokens_ready, 1)

            def turn_tokens(t, highs):
                for h in range(2):
                    half = HK // 2
                    bank = 2 * (t % 2) + h
                    s = slice(t * P, (t + 1) * P)
                    dve.wait_ge(operand_hi, highs + h + 1)
                    dve.tensor_tensor(tok[1][:, h * half:(h + 1) * half, s],
                                      banks[bank][:, :].rearrange("p (k n) -> p k n", n=P),
                                      tok[0][:, h * half:(h + 1) * half, s], ALU.subtract).then_inc(bank_emptied[bank], 1)

            def read_gate(b, c):
                if c < GC - 1:
                    for t in range(TILES):
                        bank, value = emptied(b, ("gate", c, t))
                        dve.wait_ge(bank_emptied[bank], value)
                    parts = [(slice(4 * c, 4 * c + 4), slice(0, P))]
                else:
                    dve.wait_ge(silu_done, (b + 1) * 2 * TILES)
                    parts = [(GK - 2, slice(0, P)), (GK - 1, slice(0, LAST))]
                for i, (ks, ns) in enumerate(parts):
                    dve.tensor_scalar(positive[:, ks, :, ns], mag[:, ks, :, ns], 0.0, 2.0, ALU.is_ge,
                                      ALU.mult).then_inc(signs_done, 1)
                    dve.wait_ge(signs_done, b * (GC + 1) + c + i + 1)
                    bits = mag[:, ks, :, ns].bitcast(I32)
                    dve.tensor_scalar(bits, bits, 0x7FFFFFFF, None, ALU.bitwise_and).then_inc(mag_ready, 1)

            def read_logits(b):
                for t in range(TILES):
                    bank = USE[("gate", GC - 1, t)][0]
                    dve.max(top[:, t, :], banks[bank][:, TAIL:TAIL + EXPERTS]).then_inc(route_ready, 1)
                dve.wait_ge(route_ready, b * (TILES + 1) + TILES)
                dve.tensor_tensor(route[:, :], top[:, :, 0], top[:, :, 1], ALU.add).then_inc(route_ready, 1)

            def read_step(b, name):
                kind, i = name
                if kind == "gate":
                    read_gate(b, i)
                    if i == GC - 1:
                        read_logits(b)
                        dve.memset(mag[:, GK - 1, :, LAST:P], -1.0).then_inc(mag_ready, 1)
                        dve.memset(prod[:, GK - 1, :, LAST:P], 0.0).then_inc(mag_ready, 1)
                        for t in range(TILES):
                            bank = USE[("gate", GC - 1, t)][0]
                            for ks, ns, first in ((GK - 2, slice(0, P), TAIL + EXPERTS),
                                                  (GK - 1, slice(0, LAST), TAIL + EXPERTS + P)):
                                ins = dve.scalar_tensor_tensor(
                                    out=prod[:, ks, t, ns], in0=positive[:, ks, t, ns], scalar=-1.0,
                                    in1=banks[bank][:, first:first + ns.stop], op0=ALU.add, op1=ALU.mult)
                                ins.then_inc(bank_emptied[bank] if ks == GK - 1 else kept, 1)
                for t in range(TILES):
                    key = (*name, t)
                    bank, value = USE[key][0], emptied(b, key)[1]
                    cols = slice(i % 2 * N, (i % 2 + 1) * N)
                    if kind == "latent":
                        dve.wait_ge(operand_hi, highs(b, kind, t + 1))
                        dve.tensor_tensor(latent[1][:, t, :], banks[bank][:, :], latent[0][:, t, :],
                                          ALU.subtract).then_inc(bank_emptied[bank], 1)
                    if kind == "shared":
                        dve.wait_ge(bank_filled, filled(b, key))
                        over_bank, over_value = emptied(b, ("routed" if i < 2 else "shared", i % 2, t))
                        dve.wait_ge(bank_emptied[over_bank], over_value)
                        dve.tensor_tensor(acc[:, t, cols], banks[bank][:, :], acc[:, t, cols],
                                          ALU.add).then_inc(bank_emptied[bank], 1)
                    if kind == "up":
                        dve.wait_ge(bank_filled, filled(b, key))
                        dve.scalar_tensor_tensor(out=prod[:, 4 * i:4 * i + 4, t, :],
                                                 in0=positive[:, 4 * i:4 * i + 4, t, :], scalar=-1.0,
                                                 in1=banks[bank][:, :].rearrange("p (k n) -> p k n", n=P),
                                                 op0=ALU.add, op1=ALU.mult).then_inc(bank_emptied[bank], 1)

            def settle(b, k):
                at = b * SEARCHES + searched(k) + 1 + NV
                dve.wait_ge(counted, (b * BITS + k + 1) * NS)
                dve.wait_ge(search, at)
                dve.scalar_tensor_tensor(out=step[:, :], in0=cnt[:, :], scalar=float(PAD + 1), in1=cand[:, :],
                                         op0=ALU.is_le, op1=ALU.mult).then_inc(search, 1)
                dve.wait_ge(search, at + 1)
                dve.tensor_tensor(thr[:, :], thr[:, :], step[:, :], ALU.max).then_inc(search, 1)
                dve.wait_ge(search, at + 2)

            def search_bit(b, k):
                at = b * SEARCHES + searched(k)
                dve.wait_ge(search, at)
                dve.tensor_scalar(cand[:, :].bitcast(I32), thr[:, :].bitcast(I32), 1 << (BITS - 1 - k), None,
                                  ALU.bitwise_or).then_inc(search, 1)
                for i, t in enumerate(VECTOR_TILES):
                    dve.wait_ge(search, at + 1 + i)
                    dve.tensor_scalar(junk_v[:, :, :], mag[:, :, t, :], cand[:, t:t + 1], float(1 - (GATED - KEPT)),
                                      ALU.is_lt, ALU.add, accum_out=cnt[:, t:t + 1]).then_inc(search, 1)

            def drop_ties(b):
                at = b * SEARCHES + searched(BITS)
                for t in range(TILES):
                    dve.wait_ge(search, at + t)
                    dve.tensor_scalar(junk_v[:, :, :], mag[:, :, t, :], thr[:, t:t + 1], None, ALU.is_ge, ALU.add,
                                      accum_out=cnt[:, t:t + 1]).then_inc(search, 1)
                dve.wait_ge(search, at + TILES)
                dve.tensor_scalar(extra[:, :], cnt[:, :], -float(KEPT), None, ALU.add).then_inc(search, 1)
                dve.wait_ge(search, at + TILES + 1)
                dve.tensor_reduce(most[:, 0:1], extra[:, :], AX.X, ALU.max).then_inc(search, 1)
                dve.wait_ge(search, at + TILES + 2)
                dve.transpose(most_t[:, :], most[:, :]).then_inc(search, 1)
                dve.wait_ge(search, at + TILES + 3)
                dve.tensor_reduce(ties[:, :], most_t[:, :], AX.X, ALU.max).then_inc(search, 1)
                dve.drain()
                excess = sum(dve.value_load(ties[q:q + 1, 0:1], min_val=0, max_val=GATED) for q in range(0, P, 32))
                with dve.If(excess > 0):
                    dve.scalar_tensor_tensor(out=cand[:, :], in0=thr[:, :], scalar=0.7 * 2.0 ** -23, in1=thr[:, :],
                                             op0=ALU.mult, op1=ALU.add)
                    for t in range(TILES):
                        dve.drain()
                        dve.tensor_scalar(junk_v[:, :, :], mag[:, :, t, :], cand[:, t:t + 1], None, ALU.is_ge,
                                          ALU.add, accum_out=cnt[:, t:t + 1])
                    dve.drain()
                    dve.tensor_scalar(taken[:, :], cnt[:, :], float(KEPT), None, ALU.is_ge)
                    dve.tensor_scalar(neg[:, :], cnt[:, :], -float(KEPT), None, ALU.add)
                    dve.drain()
                    dve.copy_predicated(thr[:, :], taken[:, :], cand[:, :])
                    dve.copy_predicated(extra[:, :], taken[:, :], neg[:, :])
                    dve.drain()
                    dve.tensor_scalar(neg[:, :], thr[:, :], -1.0, None, ALU.mult)
                    equal = junk_v[:, :, :].rearrange("p k n -> p (k n)")
                    rank = junk_s[:, :, :].bitcast(I16).rearrange("p k n -> p (k n)")
                    for t in range(TILES):
                        dve.drain()
                        dve.tensor_scalar(junk_v[:, :, :], mag[:, :, t, :], thr[:, t:t + 1], None, ALU.is_equal)
                        dve.drain()
                        dve.tensor_tensor_scan(rank, equal, equal, 0.0, ALU.add, ALU.max)
                        dve.drain()
                        dve.scalar_tensor_tensor(out=equal, in0=rank, scalar=extra[:, t:t + 1], in1=equal,
                                                 op0=ALU.is_le, op1=ALU.mult)
                        dve.drain()
                        dve.scalar_tensor_tensor(out=mag[:, :, t, :], in0=junk_v[:, :, :], scalar=neg[:, t:t + 1],
                                                 in1=mag[:, :, t, :], op0=ALU.mult, op1=ALU.add)
                    dve.drain()

            def mask(b, g):
                ks = slice(4 * g, min(4 * g + 4, GK))
                for t in range(TILES):
                    bank, value = emptied(b, ("up", g, t) if g < GC - 1 else ("gate", g, t))
                    dve.wait_ge(bank_emptied[bank], value)
                    if g == GC - 1:
                        dve.wait_ge(kept, (b + 1) * TILES)
                    dve.scalar_tensor_tensor(out=prod[:, ks, t, :], in0=mag[:, ks, t, :], scalar=thr[:, t:t + 1],
                                             in1=prod[:, ks, t, :], op0=ALU.is_ge, op1=ALU.mult)\
                       .then_inc(masked, 1)

            def add_out(b, i):
                for t in range(TILES):
                    bank = USE[("out", i, t)][0]
                    dve.wait_ge(bank_filled, filled(b, ("out", i, t)))
                    dve.wait_ge(apply_step, (b * TILES + t + 1) * 4)
                    dve.tensor_tensor(acc[:, t, i * N:(i + 1) * N], banks[bank][:, :], acc[:, t, i * N:(i + 1) * N],
                                      ALU.add).then_inc(bank_emptied[bank], 1)

            def apply_norm(b, t):
                at = (b * TILES + t) * 4
                dve.tensor_scalar(acc[:, t, :], acc[:, t, :], mv[:, t, 0:1], rstd[:, t:t + 1], ALU.subtract,
                                  ALU.mult).then_inc(apply_step, 1)
                dve.wait_ge(apply_step, at + 1)
                dve.tensor_tensor(acc[:, t, :], acc[:, t, :], gamma_all[:, :], ALU.mult).then_inc(apply_step, 1)
                dve.wait_ge(apply_step, at + 2)
                dve.tensor_tensor(acc[:, t, :], acc[:, t, :], beta_all[:, :], ALU.add).then_inc(apply_step, 1)
                dve.wait_ge(apply_step, at + 3)
                dve.wait_ge(rows_loaded[t % 2], 16 * (2 + 4 * b + t // 2 + 1))
                dve.tensor_tensor(acc[:, t, :], acc[:, t, :], rows_of(t), ALU.add).then_inc(apply_step, 1)

            dve.sem_inc(norm_step, 1)
            dve.sem_inc(hidden_lo, 1)
            dve.memset(most[:, :], 0.0).then_inc(constants_set, 1)
            dve.wait_ge(constants_set, 1)
            normalise(0, 0, 1)
            for t in range(1, TILES):
                normalise(t, t, t // 2 + 1)
                turn_tokens(t - 1, 2 * (t - 1))
            turn_tokens(TILES - 1, 2 * (TILES - 1))
            dve.wait_ge(consts_loaded, 32)
            with dve.Fori(0, BLOCKS) as b:
                for m in range(GRANULES):
                    if m in READ_AT and READ_AT[m][0] != "hidden":
                        read_step(b, READ_AT[m])
                    if m - 1 in SQUARE_AT:
                        i, t = SQUARE_AT[m - 1]
                        n = i % 2 * TILES + t
                        dve.wait_ge(squared, b * SC * TILES + i * TILES + t + 1)
                        dve.tensor_tensor(hidden[1][:, n, :], squares[:, n, :], hidden[0][:, n, :],
                                          ALU.subtract).then_inc(hidden_lo, 1)
                    if m in READ_UP_AT:
                        read_step(b, READ_UP_AT[m])
                    if m == SEARCH_FROM:
                        dve.wait_ge(mag_ready, (b + 1) * (GC + 3))
                        dve.memset(thr[:, :], 0.0).then_inc(search, 1)
                    if m in SEARCH_AT:
                        if SEARCH_AT[m]:
                            settle(b, SEARCH_AT[m] - 1)
                        search_bit(b, SEARCH_AT[m])
                    if m == SEARCH_END:
                        settle(b, BITS - 1)
                        drop_ties(b)
                    if m in MASK_AT:
                        mask(b, MASK_AT[m])
                    for t in range(TILES):
                        if m == NORM_AT[t]:
                            for i in (2, 3):
                                bank, value = emptied(b, ("shared", i, t))
                                dve.wait_ge(bank_emptied[bank], value)
                            moments(TILES + 8 * b + t, t, acc[:, t, :])
                        if m == NORM_AT[t] + 2:
                            inverse(TILES + 8 * b + t, t)
                            apply_norm(b, t)
                        if m == TOKENS_AT[t]:
                            normalise(TILES + 8 * b + TILES + t, t, 2 + 4 * b + 2 + t // 2 + 1)
                        if m == OUT1 + TURN_AFTER[t] + RING:
                            turn_tokens(t, highs(b, "token", 2 * t))
                    if m in TURNED_AT:
                        c = TURNED_AT[m]
                        n = P if c < GK - 1 else LAST
                        bank = USE[("turn", 0, c)][0]
                        dve.wait_ge(operand_hi, highs(b, "turn", c + 1))
                        dve.tensor_tensor(prod_t[1][0:n, c, :], banks[bank][0:n, :], prod_t[0][0:n, c, :],
                                          ALU.subtract).then_inc(bank_emptied[bank], 1)
                    if m == OUT1 + RING:
                        add_out(b, 0)
                add_out(b, 1)


def kernel(**inputs):
    import concourse.bacc as bacc
    from concourse.bass_utils import run_bass_kernel_spmd

    a = {k: np.asarray(v) for k, v in inputs.items()}
    arrays = {
        "x": np.ascontiguousarray(a["L0_attn_x"].reshape(TOKENS, HID)),
        "w_gate": np.ascontiguousarray(np.concatenate(
            [a["L0_attn_w_gate"].T, a["L0_ffn_gate_w"], a["L0_attn_w_up"][GATED - TAIL:].T], axis=1)),
        "w_up": np.ascontiguousarray(a["L0_attn_w_up"][:GATED - TAIL].T),
        "w_down": np.ascontiguousarray(a["L0_attn_w_down"].T),
        "up_w": a["L0_ffn_up_w"], "down_w": a["L0_ffn_down_w"], "fc1_w": a["L0_ffn_fc1_w"],
        "expert_w": a["L0_ffn_expert_w"].T, "fc2_w": a["L0_ffn_fc2_w"],
        "gamma": a["L0_ffn_ln_gamma"].reshape(1, HID), "beta": a["L0_ffn_ln_beta"].reshape(1, HID),
    }
    nc = bacc.Bacc("TRN2", target_bir_lowering=False, num_devices=1)
    args = [nc.dram_tensor(f"{k}_dram", v.shape, F32, kind="ExternalInput").ap() for k, v in arrays.items()]
    y = nc.dram_tensor("y_dram", (TOKENS, HID), F32, kind="ExternalOutput").ap()
    routed_w = nc.dram_tensor("routed_w", (LATENT, HID), F32, kind="Internal").ap()
    program(nc, *args, routed_w, y)
    r = run_bass_kernel_spmd(nc, [{f"{k}_dram": np.ascontiguousarray(v) for k, v in arrays.items()}], core_ids=[0])
    return r.results[0]["y_dram"].reshape(a["L0_attn_x"].shape)
```

```python
from contextlib import ExitStack

import numpy as np

import concourse.bass as bass
from concourse import mybir

F32 = mybir.dt.float32
F32R = mybir.dt.float32r
I32 = mybir.dt.int32
U8 = mybir.dt.uint8
BF16 = mybir.dt.bfloat16
I16 = mybir.dt.int16
ALU = mybir.AluOpType
ACT = mybir.ActivationFunctionType
AX = mybir.AxisListType

P = 128
N = 512
TOKENS, HID = 2048, 1024
GATED, SHARED, LATENT, EXPERTS = 2752, 2048, 512, 8
KEPT = GATED - GATED // 2
EPS = 1e-5

TILES = N // P
BLOCKS = TOKENS // N
HK = HID // P
LK = LATENT // P
GK = -(-GATED // P)
LAST = GATED - (GK - 1) * P
PAD = P - LAST
assert PAD == LAST
GC = -(-GATED // N)
TAIL = GATED - (GC - 1) * N
SC = SHARED // N
RING = 4
BITS = 31
TOP_BITS = 15

STEPS = [(("gate", c), HK) for c in range(GC)]
STEPS += [(("latent", 0), HK), (("hidden", 0), HK), (("hidden", 1), HK),
          (("routed", 0), LK), (("routed", 1), LK), (("shared", 0), HK), (("shared", 1), HK),
          (("hidden", 2), HK), (("hidden", 3), HK), (("up", GC - 2), HK), (("shared", 2), HK), (("shared", 3), HK)]
STEPS += [(("up", c), HK) for c in range(GC - 2)]
STEPS += [(("out", 0), GK), (("out", 1), GK)]
GROUPS = [GC - 2, GC - 1, *range(GC - 2)]
CHUNKS = [c for g in GROUPS for c in range(4 * g, min(4 * g + 4, GK))]
START, END, SET = {}, {}, {}
_m = 0
for _s, (_name, _n) in enumerate(STEPS):
    START[_name], END[_name], SET[_name] = _m, _m + _n - 1, _s % 2
    _m += _n
GRANULES = _m
ENDS = sorted(END.values())
INNER = GRANULES - len(STEPS)

TURN_AFTER = [5, 9, 13, 17]
AHEAD = 4
TURN_LEAD = 5

FILLED, USE = {}, {}
USES = [0] * 8


def _fill(key, bank):
    FILLED[key] = len(FILLED)
    USE[key] = (bank, USES[bank])
    USES[bank] += 1


for _name, _n in STEPS[:-2]:
    if _name == STEPS[-3][0]:
        for _c in range(AHEAD):
            _fill(("turn", 0, _c), _c)
    for _t in range(TILES):
        _fill((*_name, _t), 4 * SET[_name] + _t)
for _k in range(GK):
    if _k + AHEAD < GK:
        _fill(("turn", 0, _k + AHEAD), 4 + (_k + AHEAD) % 4)
for _t in range(TILES):
    _fill(("out", 0, _t), _t)
for _t in range(TILES):
    for _h in range(2):
        _fill(("token", _t, _h), 2 * (_t % 2) + _h)
for _t in range(TILES):
    _fill(("out", 1, _t), 4 + _t)
FILLS = len(FILLED)
FIRST = [("token", 0), ("token", 1), ("weights", 0), ("token", 2), ("token", 3), ("weights", 1)]
FIRST_AT, _m = {}, 0
for _key in FIRST:
    FIRST_AT[_key] = _m
    _m += 2 if _key[0] == "token" else LK
FIRST_FILLS = _m
FIRST_USES = [2] * 8


def filled(b, key):
    return FIRST_FILLS + b * FILLS + FILLED[key] + 1


def emptied(b, key):
    bank, use = USE[key]
    return bank, 1 + FIRST_USES[bank] + b * USES[bank] + use + 1


def released(b, m):
    return RING + b * INNER + sum(1 for x in range(m + 1) if x not in ENDS)


UP0, OUT0, OUT1 = START[("up", 0)], START[("out", 0)], START[("out", 1)]
HIGH_FROM = {"latent": 0, "hidden": LK, "turn": LK + SC * TILES, "token": LK + SC * TILES + GK}
HIGHS = LK + SC * TILES + GK + 2 * TILES


def highs(b, kind, n):
    return 2 * TILES + b * HIGHS + HIGH_FROM[kind] + n


READ_AT = {END[name] + RING: name for name, _ in STEPS if name[0] in ("gate", "latent", "routed", "shared")}
READ_UP_AT = {END[("up", g)] + (2 if g == GROUPS[-1] else RING): ("up", g) for g in range(GC - 1)}
NV = TILES // 2
NS = TILES - NV
VECTOR_TILES, SCALAR_TILES = range(NV), range(NV, TILES)
SEARCH_AT = {END[("gate", GC - 1)] + RING + 1: 0}
while len(SEARCH_AT) < BITS:
    _last = max(SEARCH_AT)
    SEARCH_AT[_last + 3 + (len(SEARCH_AT) % 2 if len(SEARCH_AT) >= TOP_BITS else 0)] = len(SEARCH_AT)
SEARCH_FROM, SEARCH_END = min(SEARCH_AT), max(SEARCH_AT) + 3
MASK_AT = {max(SEARCH_END + 1 + i, END[("up", g)] + RING + 1 if g < GC - 1 else 0): g
           for i, g in enumerate(GROUPS[:-1])}
MASK_AT[OUT0 + 3] = GROUPS[-1]
GATED_AT = {OUT0 - TURN_LEAD + c: c for c in range(GK)}
TURNED_AT = {OUT0 - TURN_LEAD + 3 + c: c for c in range(AHEAD)}
TURNED_AT.update({OUT0 + c: c for c in range(AHEAD, GK)})
assert len(GATED_AT) == GK and len(MASK_AT) == GC
READ_HIDDEN_AT = {END[("hidden", i)] + RING: ("hidden", i) for i in range(SC)}
HIDDEN_AT = {END[("hidden", i)] + RING + 1 + 2 * t: (i, t) for i in range(SC) for t in range(TILES)}
GPSIMD_HI = [m for m in range(SEARCH_FROM, OUT0) if m % 4]
NORM_AT = [OUT0 + 6 + 3 * t for t in range(TILES)]
TOKENS_AT = [OUT0 + 20, OUT0 + 21, OUT1 + 10, OUT1 + 14]
RESIDUAL_LOAD = [UP0 + 2, UP0 + 3, NORM_AT[0] + 3, NORM_AT[1] + 3]
TOKENS_LOAD = [OUT0 + 14, OUT0 + 15, OUT1 + 7, OUT1 + 11]


def scalar_his(b, m):
    return b * (GRANULES - len(GPSIMD_HI)) + sum(1 for x in range(m + 1) if x not in GPSIMD_HI)


def ring_slot_free(eng, raw_loaded, granule_used, bank_filled, b, m):
    eng.wait_ge(raw_loaded[m % RING], 16 * (b * (GRANULES // RING) + m // RING + 1))
    before = m - RING
    if before == -1:
        eng.wait_ge(bank_filled, FIRST_FILLS + b * FILLS)
    elif before < 0:
        eng.wait_ge(granule_used, b * INNER + RING + before + 2)
    elif before in ENDS:
        name = next(s for s in END if END[s] == before)
        eng.wait_ge(bank_filled, filled(b, (*name, TILES - 1)))
    else:
        eng.wait_ge(granule_used, released(b, before))


MAG_STEPS = 2 * (GC - 1) + 5


def searched(k):
    return 1 + k * (3 + NV)


SEARCHES = searched(BITS) + TILES + 4


def program(nc, x, w_gate, w_up, w_down, up_w, down_w, fc1_w, expert_w, fc2_w, gamma, beta, routed_w, y):
    ctx = ExitStack()
    with ctx:
        def sb(name, shape, dt):
            return ctx.enter_context(nc.sbuf_tensor(name, shape, dt))

        def over(name, shape, dt, offset):
            return nc.alloc_sbuf_tensor_at(name, shape, dt, offset=offset)

        def sem(name):
            return ctx.enter_context(nc.semaphore(name))

        size = GK * TILES * P * 4
        acc_at = -(-nc.sbuf_base // 32) * 32
        a_at = acc_at + TILES * HID * 4
        u_at = a_at + size
        rows_at = u_at + size
        sb("regions", [P, (TILES * HID * 4 + 2 * size + 2 * HID * 4) // 4], F32)
        acc = over("acc", [P, TILES, HID], F32, acc_at)
        rows = over("rows", [P, 2, HID], F32, rows_at)
        mag = over("mag", [P, GK, TILES, P], F32, a_at)
        prod = over("prod", [P, GK, TILES, P], F32, u_at)
        prod_t = [over("prod_t0", [P, GK, N], F32R, a_at), over("prod_t1", [P, GK, N], F32R, u_at)]
        hidden = [over(f"hidden{i}", [P, HK, N], F32R, u_at + i * HK * N * 4) for i in range(2)]
        squares = over("squares", [P, HK, N], F32, u_at + HK * N * 4)
        latent = [over("latent0", [P, LK, N], F32R, u_at + 2 * HK * N * 4), over("latent1", [P, LK, N], F32R, rows_at)]
        assert 2 * HK * N + LK * N <= (GK - 2) * TILES * P
        expert_raw = over("expert_raw", [P, LK, N], F32, a_at)
        fc2_raw = over("fc2_raw", [P, LK, HID], F32, a_at + LK * N * 4)
        expert = [over(f"expert{i}", [P, LK, N], F32R, a_at + (3 + i) * LK * N * 4) for i in range(2)]
        fc2 = [over(f"fc2_{i}", [P, LK, HID], F32R, u_at + i * LK * HID * 4) for i in range(2)]

        tok = [sb(f"tok{i}", [P, HK, N], F32R) for i in range(2)]
        raw = sb("raw", [P, RING, N], F32)
        w = [sb(f"w{i}", [P, RING, N], F32R) for i in range(2)]
        positive = sb("positive", [P, GK, TILES, P], U8)
        gamma_all = sb("gamma_all", [P, HID], F32)
        beta_all = sb("beta_all", [P, HID], F32)
        ident = sb("ident", [P, P], F32)
        mag_top = sb("mag_top", [P, GK, NV, P], BF16)
        junk_v = sb("junk_v", [P, GK, P], BF16)
        junk_s = sb("junk_s", [P, GK, P], U8)
        thr = sb("thr", [P, TILES], F32)
        cand = sb("cand", [P, TILES], F32)
        cnt = sb("cnt", [P, TILES], F32)
        step = sb("step", [P, TILES], F32)
        taken = sb("taken", [P, TILES], I32)
        extra = sb("extra", [P, TILES], F32)
        most = sb("most", [P, 32], F32)
        most_t = sb("most_t", [P, 32], F32)
        ties = sb("ties", [P, 1], I32)
        neg = sb("neg", [P, TILES], F32)
        top = sb("top", [P, TILES, 8], F32)
        route = sb("route", [P, TILES], F32)
        stats = sb("stats", [P, TILES, 2, 6], F32)
        mv = sb("mv", [P, TILES, 2], F32)
        var = sb("var", [P, TILES], F32)
        std = sb("std", [P, TILES], F32)
        rstd = sb("rstd", [P, TILES], F32)
        banks = [ctx.enter_context(nc.psum_tensor(f"bank{i}", [P, N], F32)) for i in range(8)]

        raw_loaded = [sem(f"raw_loaded{i}") for i in range(RING)]
        rows_loaded = [sem(f"rows_loaded{i}") for i in range(2)]
        consts_loaded = sem("consts_loaded")
        ident_ready = sem("ident_ready")
        hi_ready = sem("hi_ready")
        lo_ready = sem("lo_ready")
        granule_used = sem("granule_used")
        bank_filled = sem("bank_filled")
        bank_emptied = [sem(f"bank_emptied{i}") for i in range(8)]
        operand_hi = sem("operand_hi")
        hidden_lo = sem("hidden_lo")
        silu_done = sem("silu_done")
        signs_done = sem("signs_done")
        mag_ready = sem("mag_ready")
        route_ready = sem("route_ready")
        search = sem("search")
        counted = sem("counted")
        squared = sem("squared")
        gpsimd_hi = sem("gpsimd_hi")
        gpsimd_slot = sem("gpsimd_slot")
        first_loaded = [sem(f"first_loaded{k}") for k in range(LK)]
        first_hi = sem("first_hi")
        first_lo = sem("first_lo")
        routed_stored = sem("routed_stored")
        kept = sem("kept")
        doubled = sem("doubled")
        masked = sem("masked")
        constants_set = sem("constants_set")
        prod_ready = sem("prod_ready")
        norm_step = sem("norm_step")
        std_ready = sem("std_ready")
        apply_step = sem("apply_step")
        tokens_ready = sem("tokens_ready")
        stored = sem("stored")

        def source(m):
            name = max((s for s in START if START[s] <= m), key=lambda s: START[s])
            (kind, i), k = name, m - START[name]
            if kind in ("gate", "up"):
                width = N if i < GC - 1 else TAIL + EXPERTS + TAIL
                src = w_gate if kind == "gate" else w_up
                return src[k * P:(k + 1) * P, i * N:i * N + width], width
            if kind == "latent":
                return fc1_w[k * P:(k + 1) * P, :], N
            if kind == "hidden":
                return up_w[k * P:(k + 1) * P, i * N:(i + 1) * N], N
            if kind == "routed":
                return routed_w[k * P:(k + 1) * P, i * N:(i + 1) * N], N
            if kind == "shared":
                k += HK * (i // 2)
                return down_w[k * P:(k + 1) * P, i % 2 * N:(i % 2 + 1) * N], N
            k = CHUNKS[k]
            return w_down[k * P:(k + 1) * P, i * N:(i + 1) * N], N

        def rows_of(t):
            return rows[:, t % 2, :]

        block = ctx.enter_context(nc.Block())

        @block.sync
        def _(sp):
            def load_granule(m):
                src, width = source(m % GRANULES)
                if m == START[("routed", 0)]:
                    sp.wait_ge(routed_stored, 32)
                sp.dma_start(raw[:, m % RING, 0:width], src).then_inc(raw_loaded[m % RING], 16)

            def load_rows(b, t):
                sp.dma_start(rows_of(t), x[bass.ds(((b % BLOCKS) * TILES + t) * P, P), :])\
                  .then_inc(rows_loaded[t % 2], 16)

            def store(b, i, t):
                s = slice(i * N, (i + 1) * N)
                bank, value = emptied(b, ("out", i, t))
                sp.wait_ge(bank_emptied[bank], value)
                sp.dma_start(y[bass.ds((b * TILES + t) * P, P), s], acc[:, t, s]).then_inc(stored, 16)

            for t in range(2):
                load_rows(0, t)
            for k in range(LK):
                sp.dma_start(expert_raw[:, k, :], expert_w[k * P:(k + 1) * P, :]).then_inc(first_loaded[k], 16)
                sp.dma_start(fc2_raw[:, k, :], fc2_w[k * P:(k + 1) * P, :]).then_inc(first_loaded[k], 16)
            for t in range(2, TILES):
                sp.wait_ge(bank_filled, FIRST_AT[("token", t - 2)] + 2)
                load_rows(0, t)
            for m in range(RING):
                load_granule(m)
            sp.dma_start(gamma_all[:, :], gamma.to_broadcast([P, HID])).then_inc(consts_loaded, 16)
            sp.dma_start(beta_all[:, :], beta.to_broadcast([P, HID])).then_inc(consts_loaded, 16)
            for h in range(2):
                s = slice(h * N, (h + 1) * N)
                for t in range(LK):
                    sp.wait_ge(bank_emptied[4 + t], 2 + h)
                sp.dma_start(routed_w[:, s].rearrange("(k p) n -> p k n", p=P), acc[:, :, s]).then_inc(routed_stored, 16)
            with sp.Fori(0, BLOCKS) as b:
                for m in range(GRANULES):
                    sp.wait_ge(lo_ready, b * GRANULES + m + 1)
                    load_granule(m + RING)
                    for t in range(TILES):
                        if m == RESIDUAL_LOAD[t]:
                            if t < 2:
                                sp.wait_ge(bank_filled, filled(b, ("routed", 1, TILES - 1)))
                            else:
                                sp.wait_ge(apply_step, b * 4 * TILES + 4 * (t - 1))
                            load_rows(b, t)
                        if m == OUT1 + RING + 2 + t:
                            store(b, 0, t)
                        if m == TOKENS_LOAD[t]:
                            if t < 2:
                                sp.wait_ge(apply_step, b * 4 * TILES + 4 * (t + 3))
                            else:
                                sp.wait_ge(bank_filled, filled(b, ("token", t - 2, 1)))
                            load_rows(b + 1, t)
                for t in range(TILES):
                    store(b, 1, t)
            for i in range(RING):
                sp.wait_ge(raw_loaded[i], 16 * (BLOCKS * GRANULES // RING + 1))
            sp.wait_ge(stored, 16 * (2 * TILES * BLOCKS + 1))

        @block.gpsimd
        def _(pool):
            pool.memset(ident[:, :], 0.0).then_inc(ident_ready, 1)
            pool.wait_ge(ident_ready, 1)
            pool.affine_select(out=ident[:, :], in_=ident[:, :], compare_op=ALU.not_equal, fill=1.0,
                               base=0, pattern=[[-1, P]], channel_multiplier=1).then_inc(ident_ready, 1)
            for h in range(2):
                for k in range(LK):
                    if h == 0:
                        pool.wait_ge(first_hi, 2 * k + 1)
                        pool.tensor_tensor(expert[1][:, k, :], expert_raw[:, k, :], expert[0][:, k, :],
                                           ALU.subtract).then_inc(first_lo, 1)
                        pool.wait_ge(first_hi, 2 * k + 2)
                    s = slice(h * N, (h + 1) * N)
                    pool.tensor_tensor(fc2[1][:, k, s], fc2_raw[:, k, s], fc2[0][:, k, s],
                                       ALU.subtract).then_inc(first_lo, 1)
            with pool.Fori(0, BLOCKS) as b:
                for m in range(GRANULES):
                    width = source(m)[1]
                    r = m % RING
                    words, hi, lo = (v[:, r, 0:width] for v in (raw, *w))
                    if m in GPSIMD_HI:
                        ring_slot_free(pool, raw_loaded, granule_used, bank_filled, b, m)
                        pool.sem_inc(gpsimd_slot, 1)
                        pool.tensor_scalar(hi, words, 1.0, 1.0, ALU.mult, ALU.mult).then_inc(gpsimd_hi, 1)
                        pool.wait_ge(gpsimd_hi, b * len(GPSIMD_HI) + GPSIMD_HI.index(m) + 1)
                    else:
                        pool.wait_ge(hi_ready, scalar_his(b, m))
                    pool.tensor_tensor(lo, words, hi, ALU.subtract).then_inc(lo_ready, 1)
                    if m in HIDDEN_AT:
                        i, t = HIDDEN_AT[m]
                        pool.wait_ge(operand_hi, highs(b, "hidden", i * TILES + t + 1))
                        n = i % 2 * TILES + t
                        pool.tensor_tensor(squares[:, n, :], squares[:, n, :], squares[:, n, :],
                                           ALU.mult).then_inc(squared, 1)
                    if m in GATED_AT:
                        c = CHUNKS[GATED_AT[m]]
                        pool.wait_ge(masked, (b * GC + GROUPS.index(c // 4) + 1) * TILES)
                        if c == GK - 1:
                            pool.tensor_tensor(prod[:, c, :, LAST:P], prod[:, c, :, 0:LAST], mag[:, c, :, 0:LAST],
                                               ALU.mult).then_inc(doubled, 1)
                            pool.wait_ge(doubled, b + 1)
                        units = slice(0, P if c < GK - 1 else LAST)
                        pool.tensor_tensor(prod[:, c, :, units], prod[:, c, :, units], mag[:, c, :, units],
                                           ALU.mult).then_inc(prod_ready, 1)

        @block.scalar
        def _(act):
            def split(b, m):
                width = source(m)[1]
                r = m % RING
                ring_slot_free(act, raw_loaded, granule_used, bank_filled, b, m)
                act.activation(w[0][:, r, 0:width], raw[:, r, 0:width], ACT.Copy).then_inc(hi_ready, 1)

            def standard(e, t):
                act.wait_ge(norm_step, 5 * e + 5)
                act.activation(std[:, t:t + 1], var[:, t:t + 1], ACT.Sqrt).then_inc(std_ready, 1)

            def count(b, k, n, t):
                act.wait_ge(search, b * SEARCHES + searched(k) + 1)
                if k or n:
                    act.wait_ge(counted, (b * BITS + k) * NS + n)
                act.activation(junk_s[:, :, :], mag[:, :, t, :], ACT.Sign, scale=-1.0,
                               bias=cand[:, t:t + 1], accum_out=cnt[:, t:t + 1]).then_inc(counted, 1)

            def turn_tokens(t, fills):
                for h in range(2):
                    act.wait_ge(bank_filled, fills[h])
                    half = HK // 2
                    act.activation(tok[0][:, h * half:(h + 1) * half, t * P:(t + 1) * P],
                                   banks[2 * (t % 2) + h][:, :].rearrange("p (k n) -> p k n", n=P),
                                   ACT.Copy).then_inc(operand_hi, 1)

            def read_step(b, name):
                kind, i = name
                if kind == "routed" and i == 0:
                    act.wait_ge(stored, 16 * (b * 2 * TILES + 1))
                    act.wait_ge(route_ready, (b + 1) * (TILES + 1))
                for t in range(TILES):
                    bank = USE[(*name, t)][0]
                    if kind == "gate":
                        act.wait_ge(bank_filled, filled(b, (*name, t)))
                        if i < GC - 1:
                            act.activation(mag[:, 4 * i:4 * i + 4, t, :],
                                           banks[bank][:, :].rearrange("p (k n) -> p k n", n=P),
                                           ACT.Silu).then_inc(bank_emptied[bank], 1)
                        else:
                            act.activation(mag[:, GK - 2, t, :], banks[bank][:, 0:P], ACT.Silu).then_inc(silu_done, 1)
                            act.activation(mag[:, GK - 1, t, 0:LAST], banks[bank][:, P:P + LAST],
                                           ACT.Silu).then_inc(silu_done, 1)
                    if kind == "latent":
                        act.wait_ge(bank_filled, filled(b, (*name, t)))
                        act.activation(latent[0][:, t, :], banks[bank][:, :], ACT.Copy).then_inc(operand_hi, 1)
                    if kind == "hidden":
                        act.wait_ge(bank_filled, filled(b, (*name, t)))
                        act.activation(squares[:, i % 2 * TILES + t, :], banks[bank][:, :],
                                       ACT.Relu).then_inc(bank_emptied[bank], 1)
                    if kind == "routed":
                        act.wait_ge(bank_filled, filled(b, (*name, t)))
                        act.activation(acc[:, t, i * N:(i + 1) * N], banks[bank][:, :], ACT.Copy,
                                       scale=route[:, t:t + 1]).then_inc(bank_emptied[bank], 1)

            def square_hidden(b, i, t):
                bank, value = emptied(b, ("hidden", i, t))
                n = i % 2 * TILES + t
                act.wait_ge(bank_emptied[bank], value)
                act.activation(hidden[0][:, n, :], squares[:, n, :], ACT.Square).then_inc(operand_hi, 1)

            act.sem_inc(stored, 16)

            def first_parts(k):
                act.wait_ge(first_loaded[k], 32)
                act.activation(expert[0][:, k, :], expert_raw[:, k, :], ACT.Copy).then_inc(first_hi, 1)
                act.activation(fc2[0][:, k, :], fc2_raw[:, k, :], ACT.Copy).then_inc(first_hi, 1)

            def first_tokens(t):
                turn_tokens(t, [FIRST_AT[("token", t)] + 1, FIRST_AT[("token", t)] + 2])

            standard(0, 0)
            standard(1, 1)
            first_parts(0)
            first_parts(1)
            first_tokens(0)
            first_parts(2)
            first_parts(3)
            first_tokens(1)
            standard(2, 2)
            standard(3, 3)
            first_tokens(2)
            first_tokens(3)
            with act.Fori(0, BLOCKS) as b:
                for m in range(GRANULES):
                    if m not in GPSIMD_HI:
                        split(b, m)
                    for at in (READ_AT, READ_HIDDEN_AT):
                        if m in at:
                            read_step(b, at[m])
                    if m in HIDDEN_AT:
                        square_hidden(b, *HIDDEN_AT[m])
                    for n, t in enumerate(SCALAR_TILES):
                        if m - n in SEARCH_AT:
                            count(b, SEARCH_AT[m - n], n, t)
                    for t in range(TILES):
                        if m == NORM_AT[t]:
                            standard(TILES + 8 * b + t, t)
                        if m == TOKENS_AT[t]:
                            standard(TILES + 8 * b + TILES + t, t)
                        if m == OUT1 + TURN_AFTER[t] + RING:
                            turn_tokens(t, [filled(b, ("token", t, h)) for h in range(2)])
                    if m in TURNED_AT:
                        i = TURNED_AT[m]
                        c, bank = CHUNKS[i], USE[("turn", 0, i)][0]
                        act.wait_ge(bank_filled, filled(b, ("turn", 0, i)))
                        act.activation(prod_t[0][:, c, :], banks[bank][:, :], ACT.Copy).then_inc(operand_hi, 1)

        @block.tensor
        def _(pe):
            def product(out, left, right, first, last):
                pe.matmul(out, left[0], right[0], start=first, stop=False)
                pe.matmul(out, left[0], right[1], start=False, stop=False)
                return pe.matmul(out, left[1], right[0], start=False, stop=last)

            def wait_bank(b, key):
                bank, value = emptied(b, key)
                pe.wait_ge(bank_emptied[bank], value - 1)

            def turn_token(t):
                for h in range(2):
                    for k in range(HK // 2):
                        last = pe.transpose(banks[2 * (t % 2) + h][:, k * P:(k + 1) * P],
                                            rows_of(t)[:, (h * HK // 2 + k) * P:(h * HK // 2 + k + 1) * P], ident[:, :])
                    last.then_inc(bank_filled, 1)

            def turn_product(b, i):
                c, bank = CHUNKS[i], USE[("turn", 0, i)][0]
                wait_bank(b, ("turn", 0, i))
                pe.wait_ge(prod_ready, b * GK + i + 1)
                for t in range(TILES):
                    last = pe.transpose(banks[bank][:, t * P:(t + 1) * P], prod[:, c, t, :], ident[:, :])
                last.then_inc(bank_filled, 1)

            def granule(b, name, k, count):
                kind, i = name
                m = START[name] + k
                width = source(m)[1]
                r = m % RING
                pe.wait_ge(lo_ready, b * GRANULES + m + 1)
                if kind == "gate" and i == 0 and k == 0:
                    for t in range(TILES):
                        pe.wait_ge(bank_emptied[t], 1 + FIRST_USES[t] + b * USES[t])
                if kind == "routed" and i == 0:
                    bank, value = emptied(b, ("latent", 0, k))
                    pe.wait_ge(bank_emptied[bank], value)
                if kind == "shared":
                    pe.wait_ge(hidden_lo, b * SC * TILES + HK * (i // 2) + k + 2)
                if kind == "out" and i == 0:
                    bank, value = emptied(b, ("turn", 0, k))
                    pe.wait_ge(bank_emptied[bank], value)
                right = [part[:, r, 0:width] for part in w]
                for t in range(TILES):
                    if k == 0:
                        wait_bank(b, (*name, t))
                    out = banks[USE[(*name, t)][0]]
                    s = slice(t * P, (t + 1) * P)
                    if kind in ("gate", "up"):
                        last = product(out[:, 0:width], [p[:, k, s] for p in tok], right, k == 0, k == count - 1)
                    elif kind in ("latent", "hidden"):
                        last = product(out[:, :], [p[:, r, s] for p in w], [p[:, k, :] for p in tok],
                                       k == 0, k == count - 1)
                    else:
                        left = {"routed": latent, "shared": hidden, "out": prod_t}[kind]
                        c = CHUNKS[k] if kind == "out" else k
                        if kind == "out" and c == GK - 1:
                            assert 0 < k < count - 1
                            pe.matmul(out[:, :], left[0][:, c, s], right[0], start=False, stop=False)
                            last = pe.matmul(out[:, :], left[0][0:LAST, c, s], right[1][0:LAST, :], start=False, stop=False)
                        else:
                            last = product(out[:, :], [p[:, c, s] for p in left], right, k == 0, k == count - 1)
                    if k == count - 1:
                        last.then_inc(bank_filled, 1)
                if k < count - 1:
                    last.then_inc(granule_used, 1)

            for s in bank_emptied:
                pe.sem_inc(s, 1)
            pe.sem_inc(granule_used, RING)
            pe.wait_ge(ident_ready, 2)
            for kind, i in FIRST:
                if kind == "token":
                    pe.wait_ge(tokens_ready, i + 1)
                    if i >= 2:
                        for h in range(2):
                            pe.wait_ge(bank_emptied[2 * (i % 2) + h], 2)
                    turn_token(i)
                else:
                    for k in range(LK):
                        pe.wait_ge(first_lo, 2 * LK + k + 1 if i else 2 * k + 2)
                        for t in range(LK):
                            if k == 0 and i:
                                pe.wait_ge(bank_emptied[4 + t], 2)
                            last = product(banks[4 + t][:, :], [p[:, k, t * P:(t + 1) * P] for p in expert],
                                           [p[:, k, i * N:(i + 1) * N] for p in fc2], k == 0, k == LK - 1)
                            if k == LK - 1:
                                last.then_inc(bank_filled, 1)
            with pe.Fori(0, BLOCKS) as b:
                for name, count in STEPS:
                    for k in range(count):
                        granule(b, name, k, count)
                        if 0 <= START[name] + k - (OUT0 - TURN_LEAD) < AHEAD:
                            turn_product(b, START[name] + k - (OUT0 - TURN_LEAD))
                        if name == ("out", 0) and k + AHEAD < GK:
                            turn_product(b, k + AHEAD)
                        if name == ("out", 1) and k in TURN_AFTER:
                            t = TURN_AFTER.index(k)
                            pe.wait_ge(tokens_ready, TILES * (b + 1) + t + 1)
                            for h in range(2):
                                wait_bank(b, ("token", t, h))
                            turn_token(t)

        @block.vector
        def _(dve):
            def moments(e, t, src):
                dve.wait_ge(norm_step, 5 * e + 1)
                for h in range(2):
                    dve.bn_stats(stats[:, t, h, :], src[:, h * N:(h + 1) * N]).then_inc(norm_step, 1)
                dve.drain()
                dve.bn_aggr(mv[:, t, :], stats[:, t, :, :]).then_inc(norm_step, 1)
                dve.wait_ge(norm_step, 5 * e + 4)
                dve.tensor_scalar(var[:, t:t + 1], mv[:, t, 1:2], EPS, None, ALU.add).then_inc(norm_step, 1)

            def inverse(e, t):
                dve.wait_ge(std_ready, e + 1)
                dve.reciprocal(rstd[:, t:t + 1], std[:, t:t + 1]).then_inc(norm_step, 1)
                dve.wait_ge(norm_step, 5 * e + 6)

            def normalise(e, t, loads):
                dve.wait_ge(rows_loaded[t % 2], 16 * loads)
                moments(e, t, rows_of(t))
                inverse(e, t)
                dve.tensor_scalar(rows_of(t), rows_of(t), mv[:, t, 0:1], rstd[:, t:t + 1], ALU.subtract,
                                  ALU.mult).then_inc(tokens_ready, 1)

            def turn_tokens(t, highs):
                for h in range(2):
                    half = HK // 2
                    bank = 2 * (t % 2) + h
                    s = slice(t * P, (t + 1) * P)
                    dve.wait_ge(operand_hi, highs + h + 1)
                    dve.tensor_tensor(tok[1][:, h * half:(h + 1) * half, s],
                                      banks[bank][:, :].rearrange("p (k n) -> p k n", n=P),
                                      tok[0][:, h * half:(h + 1) * half, s], ALU.subtract).then_inc(bank_emptied[bank], 1)

            def read_gate(b, c):
                if c < GC - 1:
                    for t in range(TILES):
                        bank, value = emptied(b, ("gate", c, t))
                        dve.wait_ge(bank_emptied[bank], value)
                    parts = [(slice(4 * c, 4 * c + 4), slice(0, P))]
                else:
                    dve.wait_ge(silu_done, (b + 1) * 2 * TILES)
                    parts = [(GK - 2, slice(0, P)), (GK - 1, slice(0, LAST))]
                for i, (ks, ns) in enumerate(parts):
                    dve.tensor_scalar(positive[:, ks, :, ns], mag[:, ks, :, ns], 0.0, 2.0, ALU.is_ge,
                                      ALU.mult).then_inc(signs_done, 1)
                    dve.wait_ge(signs_done, b * (GC + 1) + c + i + 1)
                    bits = mag[:, ks, :, ns].bitcast(I32)
                    dve.tensor_scalar(bits, bits, 0x7FFFFFFF, None, ALU.bitwise_and).then_inc(mag_ready, 1)
                if c < GC - 1:
                    top_halves(b, 4 * c, 2 * c + 1)

            def top_halves(b, k, steps):
                ks = slice(k, min(k + 4, GK))
                dve.wait_ge(mag_ready, b * MAG_STEPS + steps)
                halves = mag[:, ks, 0:NV, :].bitcast(BF16).rearrange("p k t (n h) -> p k t n h", h=2)
                dve.tensor_copy(mag_top[:, ks, :, :], halves[:, :, :, :, 1]).then_inc(mag_ready, 1)

            def read_logits(b):
                for t in range(TILES):
                    bank = USE[("gate", GC - 1, t)][0]
                    dve.max(top[:, t, :], banks[bank][:, TAIL:TAIL + EXPERTS]).then_inc(route_ready, 1)
                dve.wait_ge(route_ready, b * (TILES + 1) + TILES)
                dve.tensor_tensor(route[:, :], top[:, :, 0], top[:, :, 1], ALU.add).then_inc(route_ready, 1)

            def read_step(b, name):
                kind, i = name
                if kind == "gate":
                    read_gate(b, i)
                    if i == GC - 1:
                        read_logits(b)
                        dve.memset(mag[:, GK - 1, :, LAST:P], -1.0).then_inc(mag_ready, 1)
                        dve.memset(prod[:, GK - 1, :, LAST:P], 0.0).then_inc(mag_ready, 1)
                        top_halves(b, 4 * i, 2 * i + 4)
                        for t in range(TILES):
                            bank = USE[("gate", GC - 1, t)][0]
                            for ks, ns, first in ((GK - 2, slice(0, P), TAIL + EXPERTS),
                                                  (GK - 1, slice(0, LAST), TAIL + EXPERTS + P)):
                                ins = dve.scalar_tensor_tensor(
                                    out=prod[:, ks, t, ns], in0=positive[:, ks, t, ns], scalar=-1.0,
                                    in1=banks[bank][:, first:first + ns.stop], op0=ALU.add, op1=ALU.mult)
                                ins.then_inc(bank_emptied[bank] if ks == GK - 1 else kept, 1)
                for t in range(TILES):
                    key = (*name, t)
                    bank, value = USE[key][0], emptied(b, key)[1]
                    cols = slice(i % 2 * N, (i % 2 + 1) * N)
                    if kind == "latent":
                        dve.wait_ge(operand_hi, highs(b, kind, t + 1))
                        dve.tensor_tensor(latent[1][:, t, :], banks[bank][:, :], latent[0][:, t, :],
                                          ALU.subtract).then_inc(bank_emptied[bank], 1)
                    if kind == "shared":
                        dve.wait_ge(bank_filled, filled(b, key))
                        over_bank, over_value = emptied(b, ("routed" if i < 2 else "shared", i % 2, t))
                        dve.wait_ge(bank_emptied[over_bank], over_value)
                        dve.tensor_tensor(acc[:, t, cols], banks[bank][:, :], acc[:, t, cols],
                                          ALU.add).then_inc(bank_emptied[bank], 1)
                    if kind == "up":
                        dve.wait_ge(bank_filled, filled(b, key))
                        dve.scalar_tensor_tensor(out=prod[:, 4 * i:4 * i + 4, t, :],
                                                 in0=positive[:, 4 * i:4 * i + 4, t, :], scalar=-1.0,
                                                 in1=banks[bank][:, :].rearrange("p (k n) -> p k n", n=P),
                                                 op0=ALU.add, op1=ALU.mult).then_inc(bank_emptied[bank], 1)

            def settle(b, k):
                at = b * SEARCHES + searched(k) + 1 + NV
                dve.wait_ge(counted, (b * BITS + k + 1) * NS)
                dve.wait_ge(search, at)
                dve.scalar_tensor_tensor(out=step[:, :], in0=cnt[:, :], scalar=float(PAD + 1), in1=cand[:, :],
                                         op0=ALU.is_le, op1=ALU.mult).then_inc(search, 1)
                dve.wait_ge(search, at + 1)
                dve.tensor_tensor(thr[:, :], thr[:, :], step[:, :], ALU.max).then_inc(search, 1)
                dve.wait_ge(search, at + 2)

            def search_bit(b, k):
                at = b * SEARCHES + searched(k)
                dve.wait_ge(search, at)
                dve.tensor_scalar(cand[:, :].bitcast(I32), thr[:, :].bitcast(I32), 1 << (BITS - 1 - k), None,
                                  ALU.bitwise_or).then_inc(search, 1)
                for i, t in enumerate(VECTOR_TILES):
                    dve.wait_ge(search, at + 1 + i)
                    words = mag_top[:, :, t, :] if k < TOP_BITS else mag[:, :, t, :]
                    dve.tensor_scalar(junk_v[:, :, :], words, cand[:, t:t + 1], float(1 - (GATED - KEPT)),
                                      ALU.is_lt, ALU.add, accum_out=cnt[:, t:t + 1]).then_inc(search, 1)

            def drop_ties(b):
                at = b * SEARCHES + searched(BITS)
                for t in range(TILES):
                    dve.wait_ge(search, at + t)
                    dve.tensor_scalar(junk_v[:, :, :], mag[:, :, t, :], thr[:, t:t + 1], None, ALU.is_ge, ALU.add,
                                      accum_out=cnt[:, t:t + 1]).then_inc(search, 1)
                dve.wait_ge(search, at + TILES)
                dve.tensor_scalar(extra[:, :], cnt[:, :], -float(KEPT), None, ALU.add).then_inc(search, 1)
                dve.wait_ge(search, at + TILES + 1)
                dve.tensor_reduce(most[:, 0:1], extra[:, :], AX.X, ALU.max).then_inc(search, 1)
                dve.wait_ge(search, at + TILES + 2)
                dve.transpose(most_t[:, :], most[:, :]).then_inc(search, 1)
                dve.wait_ge(search, at + TILES + 3)
                dve.tensor_reduce(ties[:, :], most_t[:, :], AX.X, ALU.max).then_inc(search, 1)
                dve.drain()
                excess = sum(dve.value_load(ties[q:q + 1, 0:1], min_val=0, max_val=GATED) for q in range(0, P, 32))
                with dve.If(excess > 0):
                    dve.scalar_tensor_tensor(out=cand[:, :], in0=thr[:, :], scalar=0.7 * 2.0 ** -23, in1=thr[:, :],
                                             op0=ALU.mult, op1=ALU.add)
                    for t in range(TILES):
                        dve.drain()
                        dve.tensor_scalar(junk_v[:, :, :], mag[:, :, t, :], cand[:, t:t + 1], None, ALU.is_ge,
                                          ALU.add, accum_out=cnt[:, t:t + 1])
                    dve.drain()
                    dve.tensor_scalar(taken[:, :], cnt[:, :], float(KEPT), None, ALU.is_ge)
                    dve.tensor_scalar(neg[:, :], cnt[:, :], -float(KEPT), None, ALU.add)
                    dve.drain()
                    dve.copy_predicated(thr[:, :], taken[:, :], cand[:, :])
                    dve.copy_predicated(extra[:, :], taken[:, :], neg[:, :])
                    dve.drain()
                    dve.tensor_scalar(neg[:, :], thr[:, :], -1.0, None, ALU.mult)
                    equal = junk_s[:, :, :].rearrange("p k n -> p (k n)")
                    rank = junk_v[:, :, :].bitcast(I16).rearrange("p k n -> p (k n)")
                    for t in range(TILES):
                        dve.drain()
                        dve.tensor_scalar(junk_s[:, :, :], mag[:, :, t, :], thr[:, t:t + 1], None, ALU.is_equal)
                        dve.drain()
                        dve.tensor_tensor_scan(rank, equal, equal, 0.0, ALU.add, ALU.max)
                        dve.drain()
                        dve.scalar_tensor_tensor(out=equal, in0=rank, scalar=extra[:, t:t + 1], in1=equal,
                                                 op0=ALU.is_le, op1=ALU.mult)
                        dve.drain()
                        dve.scalar_tensor_tensor(out=mag[:, :, t, :], in0=junk_s[:, :, :], scalar=neg[:, t:t + 1],
                                                 in1=mag[:, :, t, :], op0=ALU.mult, op1=ALU.add)
                    dve.drain()

            def mask(b, g):
                ks = slice(4 * g, min(4 * g + 4, GK))
                for t in range(TILES):
                    bank, value = emptied(b, ("up", g, t) if g < GC - 1 else ("gate", g, t))
                    dve.wait_ge(bank_emptied[bank], value)
                    if g == GC - 1:
                        dve.wait_ge(kept, (b + 1) * TILES)
                    dve.scalar_tensor_tensor(out=prod[:, ks, t, :], in0=mag[:, ks, t, :], scalar=thr[:, t:t + 1],
                                             in1=prod[:, ks, t, :], op0=ALU.is_ge, op1=ALU.mult)\
                       .then_inc(masked, 1)

            def add_out(b, i):
                for t in range(TILES):
                    bank = USE[("out", i, t)][0]
                    dve.wait_ge(bank_filled, filled(b, ("out", i, t)))
                    dve.wait_ge(apply_step, (b * TILES + t + 1) * 4)
                    dve.tensor_tensor(acc[:, t, i * N:(i + 1) * N], banks[bank][:, :], acc[:, t, i * N:(i + 1) * N],
                                      ALU.add).then_inc(bank_emptied[bank], 1)

            def apply_norm(b, t):
                at = (b * TILES + t) * 4
                dve.tensor_scalar(acc[:, t, :], acc[:, t, :], mv[:, t, 0:1], rstd[:, t:t + 1], ALU.subtract,
                                  ALU.mult).then_inc(apply_step, 1)
                dve.wait_ge(apply_step, at + 1)
                dve.tensor_tensor(acc[:, t, :], acc[:, t, :], gamma_all[:, :], ALU.mult).then_inc(apply_step, 1)

            def apply_rest(b, t):
                at = (b * TILES + t) * 4
                dve.wait_ge(apply_step, at + 2)
                dve.tensor_tensor(acc[:, t, :], acc[:, t, :], beta_all[:, :], ALU.add).then_inc(apply_step, 1)
                dve.wait_ge(apply_step, at + 3)
                dve.wait_ge(rows_loaded[t % 2], 16 * (2 + 4 * b + t // 2 + 1))
                dve.tensor_tensor(acc[:, t, :], acc[:, t, :], rows_of(t), ALU.add).then_inc(apply_step, 1)

            def first_copy(h):
                for t in range(LK):
                    dve.wait_ge(bank_filled, FIRST_AT[("weights", h)] + t + 1)
                    dve.tensor_copy(acc[:, t, h * N:(h + 1) * N], banks[4 + t][:, :]).then_inc(bank_emptied[4 + t], 1)

            dve.sem_inc(norm_step, 1)
            dve.sem_inc(hidden_lo, 1)
            dve.memset(most[:, :], 0.0).then_inc(constants_set, 1)
            dve.wait_ge(constants_set, 1)
            normalise(0, 0, 1)
            normalise(1, 1, 1)
            turn_tokens(0, 0)
            turn_tokens(1, 2)
            normalise(2, 2, 2)
            normalise(3, 3, 2)
            first_copy(0)
            turn_tokens(2, 4)
            turn_tokens(3, 6)
            first_copy(1)
            dve.wait_ge(consts_loaded, 32)
            with dve.Fori(0, BLOCKS) as b:
                for m in range(GRANULES):
                    if m in READ_AT:
                        read_step(b, READ_AT[m])
                    if m - 1 in HIDDEN_AT:
                        i, t = HIDDEN_AT[m - 1]
                        n = i % 2 * TILES + t
                        dve.wait_ge(squared, b * SC * TILES + i * TILES + t + 1)
                        dve.tensor_tensor(hidden[1][:, n, :], squares[:, n, :], hidden[0][:, n, :],
                                          ALU.subtract).then_inc(hidden_lo, 1)
                    if m in READ_UP_AT:
                        read_step(b, READ_UP_AT[m])
                    if m == SEARCH_FROM:
                        dve.wait_ge(mag_ready, (b + 1) * MAG_STEPS)
                        dve.memset(thr[:, :], 0.0).then_inc(search, 1)
                    if m in SEARCH_AT:
                        if SEARCH_AT[m]:
                            settle(b, SEARCH_AT[m] - 1)
                        search_bit(b, SEARCH_AT[m])
                    if m == SEARCH_END:
                        settle(b, BITS - 1)
                        drop_ties(b)
                    if m in MASK_AT:
                        mask(b, MASK_AT[m])
                    for t in range(TILES):
                        if m == NORM_AT[t]:
                            for i in (2, 3):
                                bank, value = emptied(b, ("shared", i, t))
                                dve.wait_ge(bank_emptied[bank], value)
                            moments(TILES + 8 * b + t, t, acc[:, t, :])
                        if m == NORM_AT[t] + 1:
                            inverse(TILES + 8 * b + t, t)
                            apply_norm(b, t)
                        if m == NORM_AT[t] + 2:
                            apply_rest(b, t)
                        if m == TOKENS_AT[t]:
                            normalise(TILES + 8 * b + TILES + t, t, 2 + 4 * b + 2 + t // 2 + 1)
                        if m == OUT1 + TURN_AFTER[t] + RING:
                            turn_tokens(t, highs(b, "token", 2 * t))
                    if m in TURNED_AT:
                        i = TURNED_AT[m]
                        c, bank = CHUNKS[i], USE[("turn", 0, i)][0]
                        lo, n = (prod_t[1], slice(0, P)) if c < GK - 1 else (prod_t[0], slice(LAST, P))
                        dve.wait_ge(operand_hi, highs(b, "turn", i + 1))
                        dve.tensor_tensor(lo[n, c, :], banks[bank][n, :], prod_t[0][n, c, :],
                                          ALU.subtract).then_inc(bank_emptied[bank], 1)
                    if m == OUT1 + RING:
                        add_out(b, 0)
                add_out(b, 1)


def kernel(**inputs):
    import concourse.bacc as bacc
    from concourse.bass_utils import run_bass_kernel_spmd

    a = {k: np.asarray(v) for k, v in inputs.items()}
    arrays = {
        "x": np.ascontiguousarray(a["L0_attn_x"].reshape(TOKENS, HID)),
        "w_gate": np.ascontiguousarray(np.concatenate(
            [a["L0_attn_w_gate"].T, a["L0_ffn_gate_w"], a["L0_attn_w_up"][GATED - TAIL:].T], axis=1)),
        "w_up": np.ascontiguousarray(a["L0_attn_w_up"][:GATED - TAIL].T),
        "w_down": np.ascontiguousarray(np.concatenate([a["L0_attn_w_down"].T, a["L0_attn_w_down"].T[-LAST:]])),
        "up_w": a["L0_ffn_up_w"], "down_w": a["L0_ffn_down_w"], "fc1_w": a["L0_ffn_fc1_w"],
        "expert_w": a["L0_ffn_expert_w"].T, "fc2_w": a["L0_ffn_fc2_w"],
        "gamma": a["L0_ffn_ln_gamma"].reshape(1, HID), "beta": a["L0_ffn_ln_beta"].reshape(1, HID),
    }
    nc = bacc.Bacc("TRN2", target_bir_lowering=False, num_devices=1)
    args = [nc.dram_tensor(f"{k}_dram", v.shape, F32, kind="ExternalInput").ap() for k, v in arrays.items()]
    y = nc.dram_tensor("y_dram", (TOKENS, HID), F32, kind="ExternalOutput").ap()
    routed_w = nc.dram_tensor("routed_w", (LATENT, HID), F32, kind="Internal").ap()
    program(nc, *args, routed_w, y)
    r = run_bass_kernel_spmd(nc, [{f"{k}_dram": np.ascontiguousarray(v) for k, v in arrays.items()}], core_ids=[0])
    return r.results[0]["y_dram"].reshape(a["L0_attn_x"].shape)
```
